# Optimizing a Trainium2 kernel written in Bass

```python
import numpy as np
import jax
import jax.numpy as jnp

def _softmax(x, axis=-1):
    return jax.nn.softmax(x, axis=axis)

def _gelu(x):
    return jax.nn.gelu(x, approximate=True)

def _silu(x):
    return jax.nn.silu(x)

def _sigmoid(x):
    return jax.nn.sigmoid(x)

def _layernorm(x, axis=-1, eps=1e-05):
    m = jnp.mean(x, axis=axis, keepdims=True)
    v = jnp.var(x, axis=axis, keepdims=True)
    return (x - m) / jnp.sqrt(v + eps)

def _scatter_add(tgt, idx, src, axis=0):
    return tgt.at[idx].add(src)

def _segment_sum(src, seg, n):
    return jax.ops.segment_sum(src, seg, n)
kernel_name = 'mk_adaln_d1_jaxref_r8_6a9619'

def setup_inputs(seed: int=0):
    np.random.seed(seed)
    _w = jnp.asarray

    def _L0_attn_setup():
        import jax, jax.numpy as jnp
        import numpy as np
        EPS = 1.1920929e-07

        def _rms(x):
            return x * jax.lax.rsqrt(jnp.mean(x * x, axis=-1, keepdims=True) + EPS)
        key = jax.random.key(seed)
        k0, k1, k2, k3 = jax.random.split(key, 4)
        B, S, D, DFF = (4, 256, 256, 1024)
        x = jax.random.normal(k0, (B, S, D), dtype=jnp.float32)
        w_qkv = jax.random.normal(k1, (3 * D, D), dtype=jnp.float32) * 0.02
        w_swiglu = jax.random.normal(k2, (2 * DFF, D), dtype=jnp.float32) * 0.02
        w_out = jax.random.normal(k3, (D, DFF), dtype=jnp.float32) * 0.02
        return {'x': x, 'w_qkv': w_qkv, 'w_swiglu': w_swiglu, 'w_out': w_out}
    _L0_attn_in = _L0_attn_setup()

    def _L0_ffn_setup():
        import jax, jax.numpy as jnp
        import numpy as np
        DIM_IN = 256
        DIM_HIDDEN = 1024
        key = jax.random.key(seed)
        k_x, k_g, k_u, k_d = jax.random.split(key, 4)
        s_in = 1.0 / np.sqrt(DIM_IN)
        s_hid = 1.0 / np.sqrt(DIM_HIDDEN)
        x = jax.random.normal(k_x, (4, 256, DIM_IN), dtype=jnp.float32)
        w_gate = jax.random.uniform(k_g, (DIM_HIDDEN, DIM_IN), jnp.float32, -s_in, s_in)
        w_up = jax.random.uniform(k_u, (DIM_HIDDEN, DIM_IN), jnp.float32, -s_in, s_in)
        w_down = jax.random.uniform(k_d, (DIM_IN, DIM_HIDDEN), jnp.float32, -s_hid, s_hid)
        return {'x': x, 'w_gate': w_gate, 'w_up': w_up, 'w_down': w_down}
    _L0_ffn_in = _L0_ffn_setup()
    _L0_c = _w((lambda *s: np.random.randn(*s).astype(np.float32) * 0.05)(16, 256))
    _L0_wmod = _w((lambda *s: np.random.randn(*s).astype(np.float32) * 0.05)(256, 6 * 256) * 256 ** (-0.5))
    _d = {'L0_attn_x': _L0_attn_in['x'], 'L0_attn_w_qkv': _L0_attn_in['w_qkv'], 'L0_attn_w_swiglu': _L0_attn_in['w_swiglu'], 'L0_attn_w_out': _L0_attn_in['w_out'], 'L0_ffn_w_gate': _L0_ffn_in['w_gate'], 'L0_ffn_w_up': _L0_ffn_in['w_up'], 'L0_ffn_w_down': _L0_ffn_in['w_down'], 'L0_c': _L0_c, 'L0_wmod': _L0_wmod}
    _x0 = _d['L0_attn_x']
    _d['L0_attn_x'] = jax.random.normal(jax.random.fold_in(jax.random.key(seed), 1), (16, 256, 256), dtype=_x0.dtype)
    del _x0
    return _d

def reference(L0_attn_x, L0_attn_w_qkv, L0_attn_w_swiglu, L0_attn_w_out, L0_ffn_w_gate, L0_ffn_w_up, L0_ffn_w_down, L0_c, L0_wmod):

    def _L0_attn_ref(x, w_qkv, w_swiglu, w_out):
        import jax, jax.numpy as jnp
        import numpy as np
        EPS = 1.1920929e-07

        def _rms(x):
            return x * jax.lax.rsqrt(jnp.mean(x * x, axis=-1, keepdims=True) + EPS)
        qkv = _rms(x) @ w_qkv.T
        q, k, v = jnp.split(qkv, 3, axis=-1)
        q = _rms(q)
        k = _rms(k)
        w = jnp.exp(k)
        kv_cum = jnp.cumsum(w * v, axis=1)
        w_cum = jnp.cumsum(w, axis=1)
        y = jax.nn.sigmoid(q) * (kv_cum / (w_cum + 1e-06))
        uv = y @ w_swiglu.T
        u, g = jnp.split(uv, 2, axis=-1)
        return x + u * jax.nn.silu(g) @ w_out.T

    def _L0_ffn_ref(x, w_gate, w_up, w_down):
        import jax, jax.numpy as jnp
        import numpy as np
        DIM_IN = 256
        DIM_HIDDEN = 1024
        gate = jnp.einsum('bsd,hd->bsh', x, w_gate)
        up = jnp.einsum('bsd,hd->bsh', x, w_up)
        gated = jax.nn.silu(gate) * up
        return jnp.einsum('bsh,dh->bsd', gated, w_down)
    x = L0_attn_x
    mod = (_silu(L0_c) @ L0_wmod).reshape(L0_c.shape[0], 6, 1, -1)
    sa, ca, ga, sb, cb, gb = (mod[:, 0], mod[:, 1], mod[:, 2], mod[:, 3], mod[:, 4], mod[:, 5])
    ga = (2 * (ga >= 0) - 1) * jnp.maximum(jnp.abs(ga), 0.25)
    gb = (2 * (gb >= 0) - 1) * jnp.maximum(jnp.abs(gb), 0.25)
    h = _layernorm(x, axis=-1) * (1 + ca) + sa
    x = x + ga * _L0_attn_ref(h, L0_attn_w_qkv, L0_attn_w_swiglu, L0_attn_w_out)
    h = _layernorm(x, axis=-1) * (1 + cb) + sb
    x = x + gb * _L0_ffn_ref(h, L0_ffn_w_gate, L0_ffn_w_up, L0_ffn_w_down)
    return x

_drawn_inputs = setup_inputs


def setup_inputs(seed=0):
    import zlib

    import numpy as np

    out = dict(_drawn_inputs(seed))
    spreads = {}
    factors = {'L0_attn_w_qkv': 8.0,
     'L0_attn_w_swiglu': 8.0,
     'L0_attn_w_out': 8.0,
     'L0_ffn_w_gate': 5.331,
     'L0_ffn_w_up': 5.071,
     'L0_ffn_w_down': 5.069}
    for name, (base, spread) in spreads.items():
        noise = np.random.default_rng([zlib.crc32(name.encode()), seed]).standard_normal(out[name].shape)
        drawn = base * np.exp(spread * noise) if base else spread * noise
        out[name] = jnp.asarray(drawn.astype(out[name].dtype))
    for name, factor in factors.items():
        out[name] = (out[name] * factor).astype(out[name].dtype)
    return out
```

```python
from contextlib import ExitStack

import concourse.bass as bass
from concourse import mybir

P = 128
F32 = mybir.dt.float32
F32R = mybir.dt.float32r
ACT = mybir.ActivationFunctionType
ALU = mybir.AluOpType

NBATCH, SEQ, D, HID = 16, 256, 256, 1024
BPB = 2
TOK = BPB * SEQ
NBLK = NBATCH // BPB
TILES = TOK // P
TPB = SEQ // P
KD = D // P
HT = HID // P
PAIRS = 2 * HT
EPS_LN = 1e-5
EPS_RMS = 1.1920929e-07
EPS_DEN = 1e-6

QKV0 = 0
SW0 = QKV0 + KD * 3 * D
WO0 = SW0 + KD * 2 * HID
GU0 = WO0 + HT * D
DN0 = GU0 + KD * 2 * HID
WCOLS = DN0 + HT * D
CH = 512
NCH = WCOLS // CH
NST = 3
NAB = 4
NACT = 2


def chunks_to(col):
    return -(-col // CH)


def adaln_kernel(nc, x_dram, xT_dram, w_dram, cT_dram, wmod_dram, out_dram):
    rows_dram = nc.dram_tensor("mod_rows", (2, NBATCH, 2 * D), F32).ap()
    x_blk = x_dram.rearrange("(i b) (t p) d -> i p (b t) d", b=BPB, p=P)

    with ExitStack() as ctx:
        def sb(name, shape, dt=F32):
            return ctx.enter_context(nc.sbuf_tensor(name, shape, dt))

        def sem(name):
            return ctx.enter_context(nc.semaphore(name))

        w_hi = sb("w_hi", [P, WCOLS], F32R)
        w_lo = sb("w_lo", [P, WCOLS], F32R)
        stage = sb("stage", [P, NST, CH])
        ident = sb("ident", [P, P])
        tri = sb("tri", [P, P], F32R)
        ones = sb("ones", [P, P], F32R)
        neg_half = sb("neg_half", [P, 8])
        c_sb = sb("c_sb", [P, KD, NBATCH])
        c_th = sb("c_th", [P, KD, NBATCH])
        gate_raw = sb("gate_raw", [P, 2 * KD, NBATCH])
        gate_abs = sb("gate_abs", [P, 2 * KD, NBATCH])
        gate_sgn = sb("gate_sgn", [P, 2 * KD, NBATCH])
        gates = sb("gates", [P, 2 * KD, NBATCH])
        gates_s = sb("gates_s", [P, 2 * KD, NBATCH])
        rows_sb = sb("rows_sb", [NBATCH, 2, 2 * D])
        rows = sb("rows", [P, BPB, 2 * D])
        x_sb = sb("x_sb", [P, TILES, D])
        base = sb("base", [P, 2, KD, TOK])
        hy = sb("hy", [P, TILES, D])
        hT_hi = sb("hT_hi", [P, KD, TOK], F32R)
        hT_lo = sb("hT_lo", [P, KD, TOK], F32R)
        tok = sb("tok", [P, TILES, 3 * D])
        ww_hi = sb("ww_hi", [P, TPB, 2 * D], F32R)
        ww_lo = sb("ww_lo", [P, TPB, 2 * D], F32R)
        den = sb("den", [P, 2, D])
        yT_hi = sb("yT_hi", [P, KD, TOK], F32R)
        yT_lo = sb("yT_lo", [P, KD, TOK], F32R)
        act = sb("act", [P, NACT, TOK])
        a_hi = sb("a_hi", [P, NAB, TOK], F32R)
        a_lo = sb("a_lo", [P, NAB, TOK], F32R)
        x1T = sb("x1T", [P, KD, TOK])
        junk = sb("junk", [P, 2, D])
        bn1 = sb("bn1", [P, TILES, 6])
        mv1 = sb("mv1", [P, TILES, 2])
        var1 = sb("var1", [P, TILES])
        rstd1 = sb("rstd1", [P, TILES])
        bn2 = sb("bn2", [P, TILES, 6])
        mv2 = sb("mv2", [P, TILES, 2])
        var2 = sb("var2", [P, TILES])
        rstd2 = sb("rstd2", [P, TILES])
        hsq = sb("hsq", [P, TILES])
        ms = sb("ms", [P, TILES])
        ems = sb("ems", [P, TILES, 2])
        r1 = sb("r1", [P, TILES])
        qk_sq = sb("qk_sq", [P, TILES, 2])
        qk_arg = sb("qk_arg", [P, TILES, 2])
        rqk = sb("rqk", [P, TILES, 2])

        bank = [ctx.enter_context(nc.psum_tensor(f"bank{k}", [P, 512], F32)) for k in range(8)]
        up_ps = [bank[0], bank[2]]
        gt_ps = [bank[1], bank[3]]
        acc = [bank[4], bank[5]]
        mps = [bank[6], bank[7]]

        st_loaded = [sem(f"st_loaded{k}") for k in range(NST)]
        c_loaded = sem("c_loaded")
        wmod_loaded = sem("wmod_loaded")
        x_loaded = sem("x_loaded")
        xT_loaded = sem("xT_loaded")
        rows_stored = sem("rows_stored")
        rows1_loaded = sem("rows1_loaded")
        rows2_loaded = sem("rows2_loaded")
        out_stored = sem("out_stored")
        stats_seen = sem("stats_seen")
        cst_made = sem("cst_made")
        cst_ready = sem("cst_ready")
        cth_ready = sem("cth_ready")
        silu_ready = sem("silu_ready")
        mod_ps = sem("mod_ps")
        mod_step = sem("mod_step")
        rows_ready = sem("rows_ready")
        gates_ready = sem("gates_ready")
        whi_ready = sem("whi_ready")
        wlo_ready = sem("wlo_ready")
        bn1_done = sem("bn1_done")
        mv1_done = sem("mv1_done")
        var1_ready = sem("var1_ready")
        rstd1_ready = sem("rstd1_ready")
        h_part = sem("h_part")
        h_done = sem("h_done")
        hsq_ready = sem("hsq_ready")
        ms_ready = sem("ms_ready")
        ems_ready = sem("ems_ready")
        r1_ready = sem("r1_ready")
        hT_ps = sem("hT_ps")
        hThi_ready = sem("hThi_ready")
        hTlo_ready = sem("hTlo_ready")
        base_done = sem("base_done")
        qkv_ps = sem("qkv_ps")
        qk_out = sem("qk_out")
        v_out = sem("v_out")
        sq_done = sem("sq_done")
        arg_ready = sem("arg_ready")
        rqk_ready = sem("rqk_ready")
        w_ready = sem("w_ready")
        thq_ready = sem("thq_ready")
        wv_ready = sem("wv_ready")
        wwhi_ready = sem("wwhi_ready")
        wwlo_ready = sem("wwlo_ready")
        cum_ps = sem("cum_ps")
        den_ready = sem("den_ready")
        rec_done = sem("rec_done")
        cum_used = sem("cum_used")
        y_ready = sem("y_ready")
        yT_ps = sem("yT_ps")
        yThi_ready = sem("yThi_ready")
        yTlo_ready = sem("yTlo_ready")
        pair_ps = sem("pair_ps")
        th_ready = sem("th_ready")
        tg_done = sem("tg_done")
        a_ready = sem("a_ready")
        ahi_ready = sem("ahi_ready")
        alo_ready = sem("alo_ready")
        acc_done = sem("acc_done")
        x1_ready = sem("x1_ready")
        x1_ps = sem("x1_ps")
        bn2_done = sem("bn2_done")
        mv2_done = sem("mv2_done")
        var2_ready = sem("var2_ready")
        rstd2_ready = sem("rstd2_ready")
        h2_part = sem("h2_part")
        h2_done = sem("h2_done")
        h2T_ps = sem("h2T_ps")
        h2Thi_ready = sem("h2Thi_ready")
        h2Tlo_ready = sem("h2Tlo_ready")
        out_ready = sem("out_ready")

        def by_feat(b):
            return b[:, :].rearrange("p (f t) -> p f t", f=KD)

        def by_tile(b):
            return b[:, :].rearrange("p (t d) -> p t d", t=TPB)

        def later(i):
            return not isinstance(i, int) or i > 0

        def cols(e):
            return slice(e * SEQ, (e + 1) * SEQ)

        block = ctx.enter_context(nc.Block())

        @block.sync
        def _(sp):
            def load_chunk(c):
                if c >= NST:
                    sp.wait_ge(whi_ready, c - NST + 1)
                    sp.wait_ge(wlo_ready, c - NST + 1)
                sp.dma_start(stage[:, c % NST, :], w_dram[:, c * CH:(c + 1) * CH]).then_inc(st_loaded[c % NST], 16)

            def load_x(n):
                sp.dma_start(x_sb[:, :, :], x_blk[n]).then_inc(x_loaded, 16)

            def load_xT(n):
                sp.dma_start(base[:, n % 2, :, :], xT_dram[n]).then_inc(xT_loaded, 16)

            def load_rows(which, n, loaded):
                src = rows_dram[which, bass.ds(n * BPB, BPB), :] if not isinstance(n, int) \
                    else rows_dram[which, n * BPB:(n + 1) * BPB, :]
                sp.dma_start(rows[:, :, :], src.partition_broadcast(P)).then_inc(loaded, 16)

            def body(i, more):
                n = i + 1
                if n_is_block(n):
                    if later(i):
                        sp.wait_ge(h2_done, TILES * i)
                    load_rows(0, n, rows1_loaded)
                if later(i):
                    store(i - 1)
                if n_is_block(n):
                    sp.wait_ge(h_done, TILES * (n + 1))
                load_rows(1, i, rows2_loaded)
                if more:
                    load_x(i + 2)
                    sp.wait_ge(x1_ready, 4 * i + 4)
                    load_xT(i + 2)

            def n_is_block(n):
                return not isinstance(n, int) or n < NBLK

            def store(i):
                sp.wait_ge(out_ready, 4 * i + 4)
                sp.dma_start(out_dram[i], x1T[:, :, :]).then_inc(out_stored, 16)

            sp.dma_start(c_sb[:, :, :], cT_dram).then_inc(c_loaded, 16)
            sp.dma_start(tok[:, :, :].rearrange("p t d -> p (t d)"), wmod_dram).then_inc(wmod_loaded, 16)
            load_x(0)
            for c in range(NST):
                load_chunk(c)
            load_xT(0)
            sp.wait_ge(rows_stored, 16)
            load_rows(0, 0, rows1_loaded)
            for c in range(NST, NCH):
                load_chunk(c)
                if c == 11:
                    sp.wait_ge(h_done, TILES)
                    load_x(1)
                    load_xT(1)
            sp.wait_ge(rows_stored, 32)
            body(0, True)
            with sp.Fori(1, NBLK - 2) as i:
                body(i, True)
            body(NBLK - 2, False)
            body(NBLK - 1, False)
            store(NBLK - 1)
            sp.wait_ge(out_stored, 16 * NBLK)

        @block.gpsimd
        def _(pool):
            def inv_sqrt(out, arg, n, ready):
                pool.tensor_tensor(out, arg, neg_half[:, 0:n], ALU.pow).then_inc(ready, 1)

            def a_lo_part(q, k):
                pool.wait_ge(a_ready, q + 1)
                pool.wait_ge(ahi_ready, q + 1)
                pool.tensor_tensor(a_lo[:, k % NAB, :], act[:, k % NACT, :], a_hi[:, k % NAB, :].bitcast(F32),
                                   ALU.subtract).then_inc(alo_ready, 1)

            def ln1_scale(n):
                pool.wait_ge(var1_ready, n + 1)
                inv_sqrt(rstd1[:, :], var1[:, :], TILES, rstd1_ready)

            def rms_scale(n):
                pool.wait_ge(ms_ready, n + 1)
                inv_sqrt(r1[:, :], ms[:, :], TILES, r1_ready)

            def ln2_scale(i, e):
                pool.wait_ge(var2_ready, BPB * i + e + 1)
                t = slice(TPB * e, TPB * e + TPB)
                inv_sqrt(rstd2[:, t], var2[:, t], TPB, rstd2_ready)

            def qk_scale(n, e):
                pool.wait_ge(arg_ready, 2 * (BPB * n + e) + 2)
                a = qk_arg[:, :, :].rearrange("p t s -> p (t s)")
                r = rqk[:, :, :].rearrange("p t s -> p (t s)")
                w = 2 * TPB
                inv_sqrt(r[:, w * e:w * e + w], a[:, w * e:w * e + w], w, rqk_ready)

            def ww_lo_part(n, e):
                for t in range(TPB):
                    tile = TPB * e + t
                    pool.wait_ge(wv_ready, TILES * n + tile + 1)
                    pool.wait_ge(wwhi_ready, TILES * n + tile + 1)
                    pool.tensor_tensor(ww_lo[:, t, :], tok[:, tile, D:3 * D], ww_hi[:, t, :].bitcast(F32),
                                       ALU.subtract).then_inc(wwlo_ready, 1)

            def body(i, last=False):
                n = i + 1
                for j in range(HT):
                    if j < HT - 1:
                        a_lo_part(PAIRS * i + j, j)
                    if not last:
                        if j == 0:
                            ln1_scale(n)
                        if j == 3:
                            rms_scale(n)
                ln2_scale(i, 0)
                ln2_scale(i, 1)
                if not last:
                    qk_scale(n, 0)
                    qk_scale(n, 1)
                    ww_lo_part(n, 0)
                for j in range(HT, PAIRS):
                    a_lo_part(PAIRS * i + j, j)
                    if j == 10 and not last:
                        ww_lo_part(n, 1)

            pool.memset(neg_half[:, :], -0.5)
            pool.memset(ident[:, :], 0.0).then_inc(cst_made, 1)
            pool.memset(hy[:, 0, 0:2 * P], 1.0).then_inc(cst_made, 1)
            pool.wait_ge(cst_made, 2)
            pool.affine_select(out=ident[:, :], in_=ident[:, :], compare_op=ALU.not_equal, fill=1.0,
                               base=0, pattern=[[-1, P]], channel_multiplier=1).then_inc(cst_made, 1)
            pool.affine_select(out=hy[:, 0, P:2 * P], in_=hy[:, 0, P:2 * P], compare_op=ALU.is_ge, fill=0.0,
                               base=0, pattern=[[1, P]], channel_multiplier=-1).then_inc(cst_made, 1)
            for r in range(2):
                pool.wait_ge(rows_ready, r + 1)
                pool.dma_start(rows_dram[r], rows_sb[:, r, :]).then_inc(rows_stored, 16)
                if r == 0:
                    pool.wait_ge(rows_stored, 16)
            ln1_scale(0)
            rms_scale(0)
            for e in range(BPB):
                qk_scale(0, e)
                ww_lo_part(0, e)
            body(0)
            with pool.Fori(1, NBLK - 1) as i:
                body(i)
            body(NBLK - 1, True)

        @block.scalar
        def _(se):
            def split_hi(c):
                se.wait_ge(st_loaded[c % NST], 16 * (c // NST + 1))
                se.activation(w_hi[:, c * CH:(c + 1) * CH], stage[:, c % NST, :], ACT.Copy).then_inc(whi_ready, 1)

            def a_hi_part(q, k):
                se.wait_ge(a_ready, q + 1)
                se.activation(a_hi[:, k % NAB, :], act[:, k % NACT, :], ACT.Copy).then_inc(ahi_ready, 1)

            def tanh(q, k):
                se.wait_ge(pair_ps, q + 1)
                if not isinstance(q, int) or q > 1:
                    se.wait_ge(alo_ready, q - 1)
                se.activation(act[:, k % NACT, :], gt_ps[k % 2][:, :], ACT.Tanh,
                              scale=0.25 if k % PAIRS < HT else 0.5).then_inc(th_ready, 1)

            def square(src, s, accum, ready, wait_for):
                se.wait_ge(*wait_for)
                se.activation(junk[:, s, :], src, ACT.Square, accum_out=accum).then_inc(ready, 1)

            def h_squares(n, e):
                for t in range(TPB * e, TPB * e + TPB):
                    se.wait_ge(h_done, TILES * n + t + 1)
                    if t > 1:
                        se.wait_ge(hsq_ready, TILES * n + t - 1)
                    elif later(n):
                        se.wait_ge(sq_done, 2 * TILES * n)
                    se.activation(junk[:, t % 2, :], hy[:, t, :], ACT.Square,
                                  accum_out=hsq[:, t:t + 1]).then_inc(hsq_ready, 1)

            def hT_hi_part(n, e):
                se.wait_ge(hT_ps, BPB * n + e + 1)
                se.activation(hT_hi[:, :, cols(e)], by_feat(mps[e]), ACT.Copy).then_inc(hThi_ready, 1)

            def qk_copy(n, t):
                se.wait_ge(qkv_ps, TILES * n + t + 1)
                if t == 0:
                    if later(n):
                        se.wait_ge(y_ready, TILES * n)
                    se.wait_ge(mod_ps, 3)
                    se.wait_ge(hsq_ready, TILES * (n + 1))
                se.activation(tok[:, t, 0:2 * D], up_ps[t % 2][:, :], ACT.Copy).then_inc(qk_out, 1)
                if t == 0:
                    se.wait_ge(r1_ready, n + 1)
                se.activation(tok[:, t, 2 * D:3 * D], gt_ps[t % 2][:, 0:D], ACT.Copy,
                              scale=r1[:, t:t + 1]).then_inc(v_out, 1)

            def qk_squares(n, t):
                se.wait_ge(qk_out, TILES * n + t + 1)
                for s in range(2):
                    if t > 0:
                        se.wait_ge(sq_done, 2 * (TILES * n + t) - 1 + s)
                    se.activation(junk[:, s, :], tok[:, t, s * D:(s + 1) * D], ACT.Square,
                                  accum_out=qk_sq[:, t, s:s + 1]).then_inc(sq_done, 1)

            def exp_tanh(n, t):
                se.wait_ge(rqk_ready, BPB * n + t // TPB + 1)
                se.wait_ge(sq_done, 2 * (TILES * n + t + 1))
                se.activation(tok[:, t, D:2 * D], tok[:, t, D:2 * D], ACT.Exp,
                              scale=rqk[:, t, 1:2]).then_inc(w_ready, 1)
                se.activation(tok[:, t, 0:D], tok[:, t, 0:D], ACT.Tanh,
                              scale=rqk[:, t, 0:1]).then_inc(thq_ready, 1)

            def ww_hi_part(n, e):
                if e:
                    se.wait_ge(cum_ps, TILES * n + TPB)
                for t in range(TPB):
                    tile = TPB * e + t
                    se.wait_ge(wv_ready, TILES * n + tile + 1)
                    se.activation(ww_hi[:, t, :], tok[:, tile, D:3 * D], ACT.Copy).then_inc(wwhi_ready, 1)

            def den_part(n, t):
                se.wait_ge(cum_ps, TILES * n + t + 1)
                if t > 1:
                    se.wait_ge(y_ready, TILES * n + t - 1)
                se.activation(den[:, t % 2, :], mps[t % 2][:, 0:D], ACT.Copy,
                              bias=EPS_DEN).then_inc(den_ready, 1)

            def yT_hi_part(n, e):
                se.wait_ge(yT_ps, BPB * n + e + 1)
                se.activation(yT_hi[:, :, cols(e)], by_feat(mps[e]), ACT.Copy).then_inc(yThi_ready, 1)

            def h2T_hi_part(i, e):
                se.wait_ge(h2T_ps, BPB * i + e + 1)
                se.activation(hT_hi[:, :, cols(e)], by_feat(acc[e]), ACT.Copy).then_inc(h2Thi_ready, 1)

            def body(i, last=False):
                n = i + 1
                q = PAIRS * i
                for j in range(1, HT):
                    tanh(q + j, j)
                    if not last:
                        if j in (3, 4):
                            h_squares(n, j - 3)
                        if j in (5, 6):
                            hT_hi_part(n, j - 5)
                    a_hi_part(q + j, j)
                if not last:
                    for t in range(3):
                        qk_copy(n, t)
                        qk_squares(n, t)
                h2T_hi_part(i, 0)
                if not last:
                    qk_copy(n, 3)
                h2T_hi_part(i, 1)
                if not last:
                    qk_squares(n, 3)
                    exp_tanh(n, 0)
                    exp_tanh(n, 1)
                    ww_hi_part(n, 0)
                for j in range(HT, PAIRS):
                    tanh(q + j, j)
                    if not last:
                        if j == 8:
                            exp_tanh(n, 2)
                            exp_tanh(n, 3)
                    a_hi_part(q + j, j)
                    if not last:
                        if j in (9, 12):
                            den_part(n, 2 * (j // 12))
                            den_part(n, 2 * (j // 12) + 1)
                        if j == 10:
                            ww_hi_part(n, 1)
                        if j in (14, 15):
                            yT_hi_part(n, j - 14)
                if not last:
                    tanh(q + PAIRS, PAIRS)
                    a_hi_part(q + PAIRS, PAIRS)

            se.wait_ge(c_loaded, 16)
            se.activation(c_th[:, :, :], c_sb[:, :, :], ACT.Tanh, scale=0.5).then_inc(cth_ready, 1)
            for c in range(3):
                split_hi(c)
            h_squares(0, 0)
            h_squares(0, 1)
            hT_hi_part(0, 0)
            hT_hi_part(0, 1)
            split_hi(3)
            split_hi(4)
            split_hi(5)
            for t in range(TILES):
                qk_copy(0, t)
                qk_squares(0, t)
            exp_tanh(0, 0)
            exp_tanh(0, 1)
            ww_hi_part(0, 0)
            exp_tanh(0, 2)
            exp_tanh(0, 3)
            split_hi(6)
            split_hi(7)
            ww_hi_part(0, 1)
            den_part(0, 0)
            den_part(0, 1)
            split_hi(8)
            split_hi(9)
            split_hi(10)
            den_part(0, 2)
            den_part(0, 3)
            yT_hi_part(0, 0)
            yT_hi_part(0, 1)
            for c in range(11, NCH):
                split_hi(c)
            tanh(0, 0)
            a_hi_part(0, 0)
            body(0)
            with se.Fori(1, NBLK - 1) as i:
                body(i)
            body(NBLK - 1, True)

        @block.vector
        def _(ve):
            def split_lo(c):
                ve.wait_ge(whi_ready, c + 1)
                ve.tensor_tensor(w_lo[:, c * CH:(c + 1) * CH], stage[:, c % NST, :],
                                 w_hi[:, c * CH:(c + 1) * CH].bitcast(F32), ALU.subtract).then_inc(wlo_ready, 1)

            def pair(q, k):
                a = act[:, k % NACT, :]
                ve.wait_ge(th_ready, q + 1)
                ve.scalar_tensor_tensor(out=a, in0=a, scalar=1.0, in1=gt_ps[k % 2][:, :],
                                        op0=ALU.add, op1=ALU.mult).then_inc(tg_done, 1)
                ve.wait_ge(tg_done, q + 1)
                ve.tensor_tensor(a, a, up_ps[k % 2][:, :], ALU.mult).then_inc(a_ready, 1)

            def a_lo_part(q, k):
                ve.wait_ge(ahi_ready, q + 1)
                ve.wait_ge(alo_ready, q)
                ve.tensor_tensor(a_lo[:, k % NAB, :], act[:, k % NACT, :], a_hi[:, k % NAB, :].bitcast(F32),
                                 ALU.subtract).then_inc(alo_ready, 1)

            def ln1_stats(n):
                ve.wait_ge(x_loaded, 16 * (n + 1))
                for t in range(TILES):
                    ve.bn_stats(bn1[:, t, :], x_sb[:, t, :]).then_inc(bn1_done, 1)
                ve.wait_ge(bn1_done, TILES * (n + 1))
                ve.sem_inc(stats_seen, 1)
                for t in range(TILES):
                    ve.bn_aggr(mv1[:, t, :], bn1[:, t, :]).then_inc(mv1_done, 1)
                ve.wait_ge(mv1_done, TILES * n + TILES)
                ve.tensor_scalar(var1[:, :], mv1[:, :, 1], EPS_LN, None, ALU.add).then_inc(var1_ready, 1)

            def ln1_h(n, e):
                if e == 0:
                    ve.wait_ge(rows1_loaded, 16 * (n + 1))
                    ve.wait_ge(rstd1_ready, n + 1)
                    if later(n):
                        ve.wait_ge(yT_ps, BPB * n)
                for t in range(TPB * e, TPB * e + TPB):
                    ve.scalar_tensor_tensor(out=hy[:, t, :], in0=x_sb[:, t, :], scalar=mv1[:, t, 0:1],
                                            in1=rows[:, e, D:2 * D], op0=ALU.subtract,
                                            op1=ALU.mult).then_inc(h_part, 1)
                for t in range(TPB * e, TPB * e + TPB):
                    ve.wait_ge(h_part, TILES * n + t + 1)
                    ve.scalar_tensor_tensor(out=hy[:, t, :], in0=hy[:, t, :], scalar=rstd1[:, t:t + 1],
                                            in1=rows[:, e, 0:D], op0=ALU.mult, op1=ALU.add).then_inc(h_done, 1)

            def rms_prep(n):
                ve.wait_ge(hsq_ready, TILES * (n + 1))
                ve.tensor_scalar(ms[:, :], hsq[:, :], 1.0 / D, EPS_RMS, ALU.mult, ALU.add).then_inc(ms_ready, 1)
                ve.wait_ge(ms_ready, n + 1)
                ve.tensor_scalar(ems[:, :, 0], ms[:, :], 4 * EPS_RMS, None, ALU.mult).then_inc(ems_ready, 1)
                ve.tensor_scalar(ems[:, :, 1], ms[:, :], EPS_RMS, None, ALU.mult).then_inc(ems_ready, 1)

            def hT_parts(n, e):
                ve.wait_ge(hThi_ready, BPB * n + e + 1)
                ve.tensor_tensor(hT_lo[:, :, cols(e)], by_feat(mps[e]), hT_hi[:, :, cols(e)].bitcast(F32),
                                 ALU.subtract).then_inc(hTlo_ready, 1)
                if e == 0:
                    ve.wait_ge(xT_loaded, 16 * (n + 1))
                for f in range(KD):
                    b = base[:, n % 2, f, cols(e)]
                    last = ve.scalar_tensor_tensor(out=b, in0=by_feat(mps[e])[:, f, :], scalar=gate_of(gates, f, n, e),
                                                   in1=b, op0=ALU.mult, op1=ALU.add)
                last.then_inc(base_done, 1)

            def gate_of(g, m, n, e):
                if isinstance(n, int):
                    return g[:, m, BPB * n + e:BPB * n + e + 1]
                return g[:, m, bass.ds(BPB * n + e, 1)]

            def qk_args(n, e):
                t = slice(TPB * e, TPB * e + TPB)
                ve.wait_ge(sq_done, 2 * (TILES * n + TPB * e + TPB))
                ve.wait_ge(ems_ready, 2 * n + 2)
                for s, f in ((0, 4.0), (1, 1.0)):
                    ve.scalar_tensor_tensor(out=qk_arg[:, t, s], in0=qk_sq[:, t, s], scalar=f / D,
                                            in1=ems[:, t, s], op0=ALU.mult, op1=ALU.add).then_inc(arg_ready, 1)

            def wv_part(n, t):
                ve.wait_ge(w_ready, TILES * n + t + 1)
                ve.wait_ge(v_out, TILES * n + t + 1)
                ve.tensor_tensor(tok[:, t, 2 * D:3 * D], tok[:, t, 2 * D:3 * D], tok[:, t, D:2 * D],
                                 ALU.mult).then_inc(wv_ready, 1)

            def y_part(n, t):
                d = den[:, t % 2, :]
                ve.wait_ge(den_ready, TILES * n + t + 1)
                ve.reciprocal(d, d).then_inc(rec_done, 1)
                ve.wait_ge(rec_done, TILES * n + t + 1)
                ve.tensor_tensor(d, d, mps[t % 2][:, D:2 * D], ALU.mult).then_inc(cum_used, 1)
                ve.wait_ge(cum_used, TILES * n + t + 1)
                ve.wait_ge(thq_ready, TILES * n + t + 1)
                ve.scalar_tensor_tensor(out=hy[:, t, :], in0=tok[:, t, 0:D], scalar=1.0, in1=d,
                                        op0=ALU.add, op1=ALU.mult).then_inc(y_ready, 1)

            def yT_lo_part(n, e):
                ve.wait_ge(yThi_ready, BPB * n + e + 1)
                ve.tensor_tensor(yT_lo[:, :, cols(e)], by_feat(mps[e]), yT_hi[:, :, cols(e)].bitcast(F32),
                                 ALU.subtract).then_inc(yTlo_ready, 1)

            def x1_part(i):
                ve.wait_ge(acc_done, 2 * i + 1)
                if later(i):
                    ve.wait_ge(out_stored, 16 * i)
                for e in range(BPB):
                    for f in range(KD):
                        ve.scalar_tensor_tensor(out=x1T[:, f, cols(e)], in0=acc[f][:, cols(e)],
                                                scalar=gate_of(gates_s, f, i, e),
                                                in1=base[:, i % 2, f, cols(e)],
                                                op0=ALU.mult, op1=ALU.add).then_inc(x1_ready, 1)

            def ln2_stats(i, e):
                ve.wait_ge(x1_ps, BPB * i + e + 1)
                ts = range(TPB * e, TPB * e + TPB)
                for t in ts:
                    ve.bn_stats(bn2[:, t, :], by_tile(mps[e])[:, t % TPB, :]).then_inc(bn2_done, 1)
                ve.wait_ge(bn2_done, TILES * i + TPB * e + TPB)
                ve.sem_inc(stats_seen, 1)
                for t in ts:
                    ve.bn_aggr(mv2[:, t, :], bn2[:, t, :]).then_inc(mv2_done, 1)
                ve.wait_ge(mv2_done, TILES * i + TPB * e + TPB)
                t = slice(TPB * e, TPB * e + TPB)
                ve.tensor_scalar(var2[:, t], mv2[:, t, 1], EPS_LN, None, ALU.add).then_inc(var2_ready, 1)

            def ln2_h(i, e):
                if e == 0:
                    ve.wait_ge(rows2_loaded, 16 * (i + 1))
                for t in range(TPB * e, TPB * e + TPB):
                    ve.scalar_tensor_tensor(out=hy[:, t, :], in0=by_tile(mps[e])[:, t % TPB, :],
                                            scalar=mv2[:, t, 0:1], in1=rows[:, e, D:2 * D],
                                            op0=ALU.subtract, op1=ALU.mult).then_inc(h2_part, 1)
                ve.wait_ge(rstd2_ready, BPB * i + e + 1)
                for t in range(TPB * e, TPB * e + TPB):
                    ve.wait_ge(h2_part, TILES * i + t + 1)
                    ve.scalar_tensor_tensor(out=hy[:, t, :], in0=hy[:, t, :], scalar=rstd2[:, t:t + 1],
                                            in1=rows[:, e, 0:D], op0=ALU.mult, op1=ALU.add).then_inc(h2_done, 1)

            def h2T_lo_part(i, e):
                ve.wait_ge(h2Thi_ready, BPB * i + e + 1)
                ve.tensor_tensor(hT_lo[:, :, cols(e)], by_feat(acc[e]), hT_hi[:, :, cols(e)].bitcast(F32),
                                 ALU.subtract).then_inc(h2Tlo_ready, 1)

            def out_part(i):
                ve.wait_ge(acc_done, 2 * i + 2)
                for e in range(BPB):
                    for f in range(KD):
                        o = x1T[:, f, cols(e)]
                        ve.scalar_tensor_tensor(out=o, in0=acc[f][:, cols(e)],
                                                scalar=gate_of(gates_s, KD + f, i, e), in1=o,
                                                op0=ALU.mult, op1=ALU.add).then_inc(out_ready, 1)

            def body(i, last=False):
                n = i + 1
                q = PAIRS * i
                for j in range(1, HT):
                    pair(q + j, j)
                    if not last:
                        if j == 1:
                            ln1_stats(n)
                        if j in (2, 3):
                            ln1_h(n, j - 2)
                        if j == 4:
                            rms_prep(n)
                        if j in (5, 6):
                            hT_parts(n, j - 5)
                a_lo_part(q + HT - 1, HT - 1)
                x1_part(i)
                ln2_stats(i, 0)
                ln2_h(i, 0)
                ln2_stats(i, 1)
                if not last:
                    qk_args(n, 0)
                ln2_h(i, 1)
                h2T_lo_part(i, 0)
                if not last:
                    qk_args(n, 1)
                h2T_lo_part(i, 1)
                if not last:
                    wv_part(n, 0)
                    wv_part(n, 1)
                for j in range(HT, PAIRS):
                    pair(q + j, j)
                    if not last:
                        if j == 8:
                            wv_part(n, 2)
                            wv_part(n, 3)
                        if j in (9, 10):
                            y_part(n, j - 9)
                        if j in (12, 13):
                            y_part(n, j - 10)
                        if j in (14, 15):
                            yT_lo_part(n, j - 14)
                if not last:
                    pair(q + PAIRS, PAIRS)
                out_part(i)

            ve.wait_ge(cth_ready, 1)
            ve.scalar_tensor_tensor(out=c_th[:, :, :], in0=c_th[:, :, :], scalar=1.0, in1=c_sb[:, :, :],
                                    op0=ALU.add, op1=ALU.mult).then_inc(silu_ready, 1)
            ve.wait_ge(cst_made, 4)
            ve.tensor_copy(ones[:, :], hy[:, 0, 0:P]).then_inc(cst_ready, 1)
            ve.tensor_copy(tri[:, :], hy[:, 0, P:2 * P]).then_inc(cst_ready, 1)
            ln1_stats(0)
            split_lo(0)
            for r in range(2):
                ve.wait_ge(mod_ps, r + 1)
                ve.tensor_scalar(rows_sb[:, r, 0:D], mps[r][0:NBATCH, 0:D], 0.5, None,
                                 ALU.mult).then_inc(mod_step, 1)
                ve.tensor_scalar(rows_sb[:, r, D:2 * D], mps[r][0:NBATCH, D:2 * D], 0.5, 1.0,
                                 ALU.mult, ALU.add).then_inc(mod_step, 1)
                ve.wait_ge(mod_step, 2 * r + 2)
                ve.engine_nop().then_inc(rows_ready, 1)
            ve.wait_ge(mod_ps, 3)
            ve.tensor_scalar(gate_raw[:, :, :].rearrange("p m b -> p (m b)"), acc[0][:, 0:2 * KD * NBATCH],
                             0.5, None, ALU.mult).then_inc(mod_step, 1)
            ve.wait_ge(mod_step, 5)
            ve.tensor_scalar(gate_sgn[:, :, :], gate_raw[:, :, :], 0.0, 2.0, ALU.is_ge,
                             ALU.mult).then_inc(mod_step, 1)
            ve.scalar_tensor_tensor(out=gate_abs[:, :, :], in0=gate_raw[:, :, :], scalar=-1.0,
                                    in1=gate_raw[:, :, :], op0=ALU.mult, op1=ALU.max).then_inc(mod_step, 1)
            ve.wait_ge(mod_step, 7)
            ve.tensor_scalar(gate_abs[:, :, :], gate_abs[:, :, :], 0.25, None, ALU.max).then_inc(mod_step, 1)
            ve.wait_ge(mod_step, 8)
            ve.scalar_tensor_tensor(out=gates[:, :, :], in0=gate_sgn[:, :, :], scalar=-1.0,
                                    in1=gate_abs[:, :, :], op0=ALU.add, op1=ALU.mult).then_inc(mod_step, 1)
            ve.wait_ge(mod_step, 9)
            ve.tensor_scalar(gates_s[:, 0:KD, :], gates[:, 0:KD, :], 1.0 / 8, None, ALU.mult).then_inc(gates_ready, 1)
            ve.tensor_scalar(gates_s[:, KD:, :], gates[:, KD:, :], 0.5, None, ALU.mult).then_inc(gates_ready, 1)
            ve.wait_ge(gates_ready, 2)
            split_lo(1)
            split_lo(2)
            ln1_h(0, 0)
            ln1_h(0, 1)
            rms_prep(0)
            hT_parts(0, 0)
            hT_parts(0, 1)
            split_lo(3)
            split_lo(4)
            split_lo(5)
            qk_args(0, 0)
            wv_part(0, 0)
            wv_part(0, 1)
            qk_args(0, 1)
            wv_part(0, 2)
            wv_part(0, 3)
            split_lo(6)
            split_lo(7)
            y_part(0, 0)
            y_part(0, 1)
            split_lo(8)
            split_lo(9)
            split_lo(10)
            y_part(0, 2)
            y_part(0, 3)
            yT_lo_part(0, 0)
            yT_lo_part(0, 1)
            for c in range(11, NCH):
                split_lo(c)
            pair(0, 0)
            body(0)
            with ve.Fori(1, NBLK - 1) as i:
                body(i)
            body(NBLK - 1, True)

        @block.tensor
        def _(pe):
            def product(out, terms):
                for k, (c, hi, lo) in enumerate(terms):
                    end = k == len(terms) - 1
                    pe.matmul(out, w_hi[:, c:c + P], hi, start=k == 0, stop=False)
                    pe.matmul(out, w_hi[:, c:c + P], lo, start=False, stop=False)
                    last = pe.matmul(out, w_lo[:, c:c + P], hi, start=False, stop=end)
                return last

            def pair(i, w0, j, k, hi, lo):
                for tk in ([cols(e) for e in range(BPB)] if j == 0 else [slice(0, TOK)]):
                    if j == 0:
                        for ready in (yThi_ready, yTlo_ready) if w0 == SW0 else (h2Thi_ready, h2Tlo_ready):
                            pe.wait_ge(ready, BPB * i + tk.start // SEQ + 1)
                    for h, ps in ((0, up_ps[k % 2]), (1, gt_ps[k % 2])):
                        last = product(ps[:, tk], [(w0 + f * 2 * HID + h * HID + j * P, hi[:, f, tk], lo[:, f, tk])
                                                   for f in range(KD)])
                last.then_inc(pair_ps, 1)

            def S(i, j):
                if later(i) or j > 1:
                    pe.wait_ge(a_ready, PAIRS * i + j - 1)
                pair(i, SW0, j, j, yT_hi, yT_lo)

            def G(i, j, first_free):
                if j == 0:
                    pe.wait_ge(whi_ready, chunks_to(DN0))
                    pe.wait_ge(wlo_ready, chunks_to(DN0))
                if j < 2 and first_free:
                    pe.wait_ge(qk_out, TILES * (i + 1) + j + 3)
                    pe.wait_ge(v_out, TILES * (i + 1) + j + 3)
                else:
                    pe.wait_ge(a_ready, PAIRS * i + HT + j - 1)
                pair(i, GU0, j, j, hT_hi, hT_lo)

            def project(i, j, ph, w0):
                q = PAIRS * i + ph * HT + j
                if j == 0:
                    pe.wait_ge(whi_ready, chunks_to(WO0 + HT * D) if ph == 0 else NCH)
                    pe.wait_ge(wlo_ready, chunks_to(WO0 + HT * D) if ph == 0 else NCH)
                    if ph == 0 and later(i):
                        pe.wait_ge(out_ready, 4 * i)
                pe.wait_ge(ahi_ready, q + 1)
                pe.wait_ge(alo_ready, q + 1)
                for f in range(KD):
                    c = w0 + j * D + f * P
                    hi, lo = a_hi[:, j % NAB, :], a_lo[:, j % NAB, :]
                    pe.matmul(acc[f][:, :], w_hi[:, c:c + P], hi, start=j == 0, stop=False)
                    pe.matmul(acc[f][:, :], w_hi[:, c:c + P], lo, start=False, stop=False)
                    last = pe.matmul(acc[f][:, :], w_lo[:, c:c + P], hi, start=False, stop=j == HT - 1)
                if j == HT - 1:
                    last.then_inc(acc_done, 1)

            def O(i, j):
                project(i, j, 0, WO0)

            def Dn(i, j):
                project(i, j, 1, DN0)

            def token_to_feature(dst, e, ready):
                for t in range(TPB):
                    for f in range(KD):
                        last = pe.transpose(by_feat(dst)[:, f, t * P:(t + 1) * P],
                                            hy[:, TPB * e + t, f * P:(f + 1) * P], ident[:, :])
                last.then_inc(ready, 1)

            def A(n, e):
                pe.wait_ge(h_done, TILES * n + TPB * (e + 1))
                token_to_feature(mps[e], e, hT_ps)

            def X(i, e):
                pe.wait_ge(x1_ready, 4 * i + 2 * (e + 1))
                for t in range(TPB):
                    for f in range(KD):
                        last = pe.transpose(by_tile(mps[e])[:, t, f * P:(f + 1) * P],
                                            x1T[:, f, (TPB * e + t) * P:(TPB * e + t + 1) * P], ident[:, :])
                last.then_inc(x1_ps, 1)

            def N(i, e):
                pe.wait_ge(h2_done, TILES * i + TPB * (e + 1))
                token_to_feature(acc[e], e, h2T_ps)

            def Q_part(t, out, c0, wd):
                for f in range(KD):
                    c = QKV0 + f * 3 * D + c0
                    hi, lo = hT_hi[:, f, t * P:(t + 1) * P], hT_lo[:, f, t * P:(t + 1) * P]
                    pe.matmul(out, hi, w_hi[:, c:c + wd], start=f == 0, stop=False)
                    pe.matmul(out, hi, w_lo[:, c:c + wd], start=False, stop=False)
                    last = pe.matmul(out, lo, w_hi[:, c:c + wd], start=False, stop=f == KD - 1)
                return last

            def Q_v(n, t):
                if t % TPB == 0:
                    pe.wait_ge(hThi_ready, BPB * n + t // TPB + 1)
                    pe.wait_ge(hTlo_ready, BPB * n + t // TPB + 1)
                Q_part(t, gt_ps[t % 2][:, 0:D], 2 * D, D)

            def Q_qk(n, t):
                Q_part(t, up_ps[t % 2][:, :], 0, 2 * D).then_inc(qkv_ps, 1)

            def Q(n, t):
                Q_v(n, t)
                Q_qk(n, t)

            def T(n, e):
                pe.wait_ge(wwhi_ready, TILES * n + TPB * (e + 1))
                pe.wait_ge(wwlo_ready, TILES * n + TPB * (e + 1))
                if e:
                    pe.wait_ge(cum_used, TILES * n + 1)
                pe.matmul(mps[0][:, :], tri[:, :], ww_hi[:, 0, :], start=True, stop=False)
                pe.matmul(mps[0][:, :], tri[:, :], ww_lo[:, 0, :], start=False, stop=True).then_inc(cum_ps, 1)
                if e:
                    pe.wait_ge(cum_used, TILES * n + 2)
                pe.matmul(mps[1][:, :], ones[:, :], ww_hi[:, 0, :], start=True, stop=False)
                pe.matmul(mps[1][:, :], ones[:, :], ww_lo[:, 0, :], start=False, stop=False)
                pe.matmul(mps[1][:, :], tri[:, :], ww_hi[:, 1, :], start=False, stop=False)
                pe.matmul(mps[1][:, :], tri[:, :], ww_lo[:, 1, :], start=False, stop=True).then_inc(cum_ps, 1)

            def Y(n, e):
                pe.wait_ge(cum_used, TILES * n + 3 + e)
                pe.wait_ge(y_ready, TILES * n + TPB * (e + 1))
                token_to_feature(mps[e], e, yT_ps)

            def body(i, last=False):
                n = i + 1
                S(i, 1)
                for j in range(2, HT):
                    S(i, j)
                    if not last and j in (4, 5):
                        A(n, j - 4)
                    O(i, j - 2)
                O(i, HT - 2)
                if not last:
                    pe.wait_ge(a_ready, PAIRS * i + HT - 1)
                    Q_v(n, 0)
                O(i, HT - 1)
                if not last:
                    Q_qk(n, 0)
                    pe.wait_ge(base_done, BPB * (n + 1))
                X(i, 0)
                X(i, 1)
                if not last:
                    pe.wait_ge(a_ready, PAIRS * i + HT)
                    Q(n, 1)
                    pe.wait_ge(qk_out, TILES * n + 1)
                    pe.wait_ge(v_out, TILES * n + 1)
                    Q(n, 2)
                N(i, 0)
                if not last:
                    pe.wait_ge(qk_out, TILES * n + 2)
                    pe.wait_ge(v_out, TILES * n + 2)
                    Q(n, 3)
                N(i, 1)
                for j in range(HT):
                    G(i, j, not last)
                    if not last:
                        if j in (1, 4):
                            T(n, j // 4)
                        if j in (6, 7):
                            Y(n, j - 6)
                    if j >= 2:
                        Dn(i, j - 2)
                Dn(i, HT - 2)
                if not last:
                    S(n, 0)
                Dn(i, HT - 1)

            wmod = tok[:, :, :].rearrange("p t d -> p (t d)").rearrange("p (k m) -> p k m", k=KD)
            pe.wait_ge(silu_ready, 1)
            pe.wait_ge(wmod_loaded, 16)
            for r in range(2):
                for k in range(KD):
                    m = pe.matmul(mps[r][0:NBATCH, :], c_th[:, k, :], wmod[:, k, 3 * D * r:3 * D * r + 2 * D],
                                  start=k == 0, stop=k == KD - 1)
                m.then_inc(mod_ps, 1)
            for g in range(2 * KD):
                c = 3 * D * (g // KD) + 2 * D + (g % KD) * P
                for k in range(KD):
                    m = pe.matmul(acc[0][:, g * NBATCH:(g + 1) * NBATCH], wmod[:, k, c:c + P], c_th[:, k, :],
                                  start=k == 0, stop=k == KD - 1)
            m.then_inc(mod_ps, 1)
            pe.wait_ge(mod_step, 4)
            A(0, 0)
            A(0, 1)
            pe.wait_ge(whi_ready, chunks_to(SW0))
            pe.wait_ge(wlo_ready, chunks_to(SW0))
            for t in range(TILES):
                if t > 1:
                    pe.wait_ge(qk_out, t - 1)
                    pe.wait_ge(v_out, t - 1)
                Q(0, t)
            pe.wait_ge(cst_ready, 2)
            pe.wait_ge(base_done, BPB)
            T(0, 0)
            T(0, 1)
            Y(0, 0)
            Y(0, 1)
            pe.wait_ge(whi_ready, chunks_to(WO0))
            pe.wait_ge(wlo_ready, chunks_to(WO0))
            pe.wait_ge(qk_out, TILES)
            pe.wait_ge(v_out, TILES)
            S(0, 0)
            body(0)
            with pe.Fori(1, NBLK - 1) as i:
                body(i)
            body(NBLK - 1, True)


def kernel(L0_attn_x, L0_attn_w_qkv, L0_attn_w_swiglu, L0_attn_w_out, L0_ffn_w_gate, L0_ffn_w_up,
           L0_ffn_w_down, L0_c, L0_wmod):
    import numpy as np
    import concourse.bacc as bacc
    from concourse.bass_utils import run_bass_kernel_spmd

    def rows_by_partition(w):
        k, m = w.shape
        return w.reshape(k // P, P, m).transpose(1, 0, 2).reshape(P, -1)

    x = np.ascontiguousarray(L0_attn_x)
    xT = x.reshape(NBLK, BPB, SEQ, KD, P).transpose(0, 4, 3, 1, 2).reshape(NBLK, P, KD, TOK)
    up_gate = np.concatenate([np.asarray(L0_ffn_w_up), np.asarray(L0_ffn_w_gate)], axis=0)
    weights = np.concatenate([
        rows_by_partition(np.asarray(L0_attn_w_qkv).T),
        rows_by_partition(np.asarray(L0_attn_w_swiglu).T),
        rows_by_partition(np.asarray(L0_attn_w_out).T),
        rows_by_partition(up_gate.T),
        rows_by_partition(np.asarray(L0_ffn_w_down).T),
    ], axis=1)
    arrays = {
        "x": x,
        "xT": np.ascontiguousarray(xT),
        "weights": np.ascontiguousarray(weights),
        "cT": np.ascontiguousarray(rows_by_partition(np.asarray(L0_c).T).reshape(P, KD, NBATCH)),
        "wmod": np.ascontiguousarray(rows_by_partition(np.asarray(L0_wmod))),
    }
    nc = bacc.Bacc("TRN2", target_bir_lowering=False, num_devices=1)
    args = [nc.dram_tensor(k, a.shape, mybir.dt.from_np(a.dtype), kind="ExternalInput").ap()
            for k, a in arrays.items()]
    out = nc.dram_tensor("outT", (NBLK, P, KD, TOK), F32, kind="ExternalOutput").ap()
    adaln_kernel(nc, *args, out)
    r = run_bass_kernel_spmd(nc, [arrays], core_ids=[0])
    outT = r.results[0]["outT"].reshape(NBLK, P, KD, BPB, SEQ)
    return np.ascontiguousarray(outT.transpose(0, 3, 4, 2, 1).reshape(NBATCH, SEQ, D))
```

```python
from contextlib import ExitStack

import concourse.bass as bass
from concourse import mybir

P = 128
F32 = mybir.dt.float32
F32R = mybir.dt.float32r
ACT = mybir.ActivationFunctionType
ALU = mybir.AluOpType

NBATCH, SEQ, D, HID = 16, 256, 256, 1024
BPB = 2
TOK = BPB * SEQ
NBLK = NBATCH // BPB
TILES = TOK // P
TPB = SEQ // P
KD = D // P
HT = HID // P
PAIRS = 2 * HT
EPS_LN = 1e-5
EPS_RMS = 1.1920929e-07
EPS_DEN = 1e-6

CH = 2 * D
GROUP = 3 * CH
QKV0 = 0
MIX0 = QKV0 + KD * 3 * D
FFN0 = MIX0 + HT // 2 * GROUP
WCOLS = FFN0 + HT // 2 * GROUP
NCH = WCOLS // CH
NCH_QKV = MIX0 // CH
NST = 3
NAB = 4
NACT = 2
LAG = 3
WARMUP = 8
SPLIT_AT = {1: (9,), 2: (10, 11), 3: (12,), 4: (13, 14), 5: (15,), 6: (16,), 7: (17, 18, 19),
            8: (20, 21), 10: (22,), 11: (23, 24), 12: (25,), 13: (26,)}


def in_col(w0, j, h, f):
    return w0 + j // 2 * GROUP + j % 2 * CH + (h * KD + f) * P


def out_col(w0, j, f):
    return w0 + j // 2 * GROUP + 2 * CH + j % 2 * D + f * P


def chunks_to(col):
    return -(-col // CH)


def adaln_kernel(nc, x_dram, xT_dram, w_dram, cT_dram, wmod_dram, out_dram):
    rows_dram = nc.dram_tensor("mod_rows", (2, NBATCH, 2 * D), F32).ap()
    x_blk = x_dram.rearrange("(i b) (t p) d -> i p (b t) d", b=BPB, p=P)

    with ExitStack() as ctx:
        def sb(name, shape, dt=F32):
            return ctx.enter_context(nc.sbuf_tensor(name, shape, dt))

        def sem(name):
            return ctx.enter_context(nc.semaphore(name))

        w_hi = sb("w_hi", [P, WCOLS], F32R)
        w_lo = sb("w_lo", [P, WCOLS], F32R)
        stage = sb("stage", [P, NST, CH])
        ident = sb("ident", [P, P])
        tri = sb("tri", [P, P], F32R)
        ones = sb("ones", [P, P], F32R)
        neg_half = sb("neg_half", [P, 8])
        c_sb = sb("c_sb", [P, KD, NBATCH])
        c_th = sb("c_th", [P, KD, NBATCH])
        c_rep = sb("c_rep", [P, KD, BPB, P])
        gate_raw = sb("gate_raw", [P, 2 * KD, NBATCH])
        gate_abs = sb("gate_abs", [P, 2 * KD, NBATCH])
        gate_sgn = sb("gate_sgn", [P, 2 * KD, NBATCH])
        gates = sb("gates", [P, 2 * KD, NBATCH])
        gates_s = sb("gates_s", [P, 2 * KD, NBATCH])
        rows_sb = sb("rows_sb", [NBATCH, 2, 2 * D])
        rows = sb("rows", [P, BPB, 2 * D])
        x_sb = sb("x_sb", [P, TILES, D])
        base = sb("base", [P, 2, KD, TOK])
        hy = sb("hy", [P, TILES, D])
        hT_hi = sb("hT_hi", [P, KD, TOK], F32R)
        hT_lo = sb("hT_lo", [P, KD, TOK], F32R)
        tok = sb("tok", [P, TILES, 3 * D])
        ww_hi = sb("ww_hi", [P, TPB, 2 * D], F32R)
        ww_lo = sb("ww_lo", [P, TPB, 2 * D], F32R)
        den = sb("den", [P, 2, D])
        yT_hi = sb("yT_hi", [P, KD, TOK], F32R)
        yT_lo = sb("yT_lo", [P, KD, TOK], F32R)
        act = sb("act", [P, NACT, TOK])
        a_hi = sb("a_hi", [P, NAB, TOK], F32R)
        a_lo = sb("a_lo", [P, NAB, TOK], F32R)
        x1T = sb("x1T", [P, KD, TOK])
        junk = sb("junk", [P, 2, D])
        bn1 = sb("bn1", [P, TILES, 6])
        mv1 = sb("mv1", [P, TILES, 2])
        var1 = sb("var1", [P, TILES])
        rstd1 = sb("rstd1", [P, TILES])
        bn2 = sb("bn2", [P, TILES, 6])
        mv2 = sb("mv2", [P, TILES, 2])
        var2 = sb("var2", [P, TILES])
        rstd2 = sb("rstd2", [P, TILES])
        hsq = sb("hsq", [P, TILES])
        ms = sb("ms", [P, TILES])
        ems = sb("ems", [P, TILES, 2])
        r1 = sb("r1", [P, TILES])
        qk_sq = sb("qk_sq", [P, TILES, 2])
        qk_arg = sb("qk_arg", [P, TILES, 2])
        rqk = sb("rqk", [P, TILES, 2])

        bank = [ctx.enter_context(nc.psum_tensor(f"bank{k}", [P, 512], F32)) for k in range(8)]
        up_ps = [bank[0], bank[2]]
        gt_ps = [bank[1], bank[3]]
        acc = [bank[4], bank[5]]
        mps = [bank[6], bank[7]]

        st_loaded = [sem(f"st_loaded{k}") for k in range(NST)]
        c_loaded = sem("c_loaded")
        wrow_loaded = [sem(f"wrow_loaded{r}") for r in range(2)]
        wgate_loaded = sem("wgate_loaded")
        x_loaded = sem("x_loaded")
        xT_loaded = sem("xT_loaded")
        rows_stored = sem("rows_stored")
        rows1_loaded = sem("rows1_loaded")
        rows2_loaded = sem("rows2_loaded")
        out_stored = sem("out_stored")
        stats_seen = sem("stats_seen")
        cst_made = sem("cst_made")
        cst_ready = sem("cst_ready")
        cth_ready = sem("cth_ready")
        silu_ready = sem("silu_ready")
        crep_ready = sem("crep_ready")
        rep_ps = sem("rep_ps")
        rep_ready = sem("rep_ready")
        gate_ps = sem("gate_ps")
        mod_ps = sem("mod_ps")
        mod_step = sem("mod_step")
        rows_ready = sem("rows_ready")
        gates_ready = sem("gates_ready")
        qkvlo_ready = sem("qkvlo_ready")
        whi_ready = sem("whi_ready")
        wlo_ready = sem("wlo_ready")
        bn1_done = sem("bn1_done")
        mv1_done = sem("mv1_done")
        var1_ready = sem("var1_ready")
        rstd1_ready = sem("rstd1_ready")
        h_part = sem("h_part")
        h_done = sem("h_done")
        hsq_ready = sem("hsq_ready")
        ms_ready = sem("ms_ready")
        ems_ready = sem("ems_ready")
        r1_ready = sem("r1_ready")
        hT_ps = sem("hT_ps")
        hThi_ready = sem("hThi_ready")
        hTlo_ready = sem("hTlo_ready")
        base_done = sem("base_done")
        qk_ps = sem("qk_ps")
        v_ps = sem("v_ps")
        qk_out = sem("qk_out")
        v_out = sem("v_out")
        sq_done = sem("sq_done")
        arg_ready = sem("arg_ready")
        rqk_ready = sem("rqk_ready")
        w_ready = sem("w_ready")
        thq_ready = sem("thq_ready")
        wv_ready = sem("wv_ready")
        wwhi_ready = sem("wwhi_ready")
        wwlo_ready = sem("wwlo_ready")
        cum_ps = sem("cum_ps")
        den_ready = sem("den_ready")
        rec_done = sem("rec_done")
        cum_used = sem("cum_used")
        y_ready = sem("y_ready")
        yT_ps = sem("yT_ps")
        yThi_ready = sem("yThi_ready")
        yTlo_ready = sem("yTlo_ready")
        pair_ps = sem("pair_ps")
        th_ready = sem("th_ready")
        tg_done = sem("tg_done")
        a_ready = sem("a_ready")
        ahi_ready = sem("ahi_ready")
        alo_ready = sem("alo_ready")
        acc_done = sem("acc_done")
        x1_ready = sem("x1_ready")
        x1_ps = sem("x1_ps")
        bn2_done = sem("bn2_done")
        mv2_done = sem("mv2_done")
        var2_ready = sem("var2_ready")
        rstd2_ready = sem("rstd2_ready")
        h2_part = sem("h2_part")
        h2_done = sem("h2_done")
        h2T_ps = sem("h2T_ps")
        h2Thi_ready = sem("h2Thi_ready")
        h2Tlo_ready = sem("h2Tlo_ready")
        out_ready = sem("out_ready")

        def by_feat(b):
            return b[:, :].rearrange("p (f t) -> p f t", f=KD)

        def by_tile(b):
            return b[:, :].rearrange("p (t d) -> p t d", t=TPB)

        def later(i):
            return not isinstance(i, int) or i > 0

        def cum_bank(n, t):
            return mps[t % TPB] if later(n) or t < TPB else (up_ps, gt_ps)[t % TPB][1]

        wrow = [base[:, 1, :, :], x1T[:, :, :]]
        wgate = act[:, 0:KD, :]

        def wait_weights(eng, col):
            eng.wait_ge(whi_ready, chunks_to(col))
            if col <= MIX0:
                eng.wait_ge(qkvlo_ready, chunks_to(col))
            else:
                eng.wait_ge(wlo_ready, chunks_to(col) - NCH_QKV)

        def cols(e):
            return slice(e * SEQ, (e + 1) * SEQ)

        block = ctx.enter_context(nc.Block())

        @block.sync
        def _(sp):
            def load_chunk(c):
                if c >= NST:
                    wait_weights(sp, (c - NST + 1) * CH)
                sp.dma_start(stage[:, c % NST, :], w_dram[:, c * CH:(c + 1) * CH]).then_inc(st_loaded[c % NST], 16)

            def load_x(n):
                sp.dma_start(x_sb[:, :, :], x_blk[n]).then_inc(x_loaded, 16)

            def load_xT(n):
                sp.dma_start(base[:, n % 2, :, :], xT_dram[n]).then_inc(xT_loaded, 16)

            def load_rows(which, n, loaded):
                src = rows_dram[which, bass.ds(n * BPB, BPB), :] if not isinstance(n, int) \
                    else rows_dram[which, n * BPB:(n + 1) * BPB, :]
                sp.dma_start(rows[:, :, :], src.partition_broadcast(P)).then_inc(loaded, 16)

            def body(i, more):
                n = i + 1
                if n_is_block(n):
                    sp.wait_ge(h2_done, TILES * i)
                    load_rows(0, n, rows1_loaded)
                store(i - 1)
                if n_is_block(n):
                    sp.wait_ge(h_done, TILES * (n + 1))
                load_rows(1, i, rows2_loaded)
                if more:
                    load_x(i + 2)
                    sp.wait_ge(x1_ready, 4 * i + 4)
                    load_xT(i + 2)

            def n_is_block(n):
                return not isinstance(n, int) or n < NBLK

            def store(i):
                sp.wait_ge(out_ready, 4 * i + 4)
                sp.dma_start(out_dram[i], x1T[:, :, :]).then_inc(out_stored, 16)

            sp.dma_start(c_sb[:, :, :], cT_dram).then_inc(c_loaded, 16)
            sp.dma_start(wrow[0], wmod_dram[0]).then_inc(wrow_loaded[0], 16)
            load_x(0)
            for c in range(NST):
                load_chunk(c)
            sp.dma_start(wgate, wmod_dram[2]).then_inc(wgate_loaded, 16)
            load_xT(0)
            sp.dma_start(wrow[1], wmod_dram[1]).then_inc(wrow_loaded[1], 16)
            for c in range(NST, 2 * NST):
                load_chunk(c)
            sp.wait_ge(h_done, TILES)
            load_x(1)
            for c in range(2 * NST, 9):
                load_chunk(c)
            sp.wait_ge(base_done, BPB)
            sp.wait_ge(mod_ps, 1)
            load_xT(1)
            for r in range(2):
                sp.wait_ge(rows_ready, r + 1)
                sp.dma_start(rows_dram[r], rows_sb[:, r, :]).then_inc(rows_stored, 16)
            for c in range(9, 12):
                load_chunk(c)
            sp.wait_ge(rows_stored, 32)
            load_rows(0, 1, rows1_loaded)
            for c in range(12, 15):
                load_chunk(c)
            sp.wait_ge(h_done, TILES * 2)
            load_rows(1, 0, rows2_loaded)
            load_x(2)
            for c in range(15, 20):
                load_chunk(c)
            sp.wait_ge(x1_ready, 4)
            load_xT(2)
            for c in range(20, NCH):
                load_chunk(c)
            with sp.Fori(1, NBLK - 2) as i:
                body(i, True)
            body(NBLK - 2, False)
            body(NBLK - 1, False)
            for f in range(KD):
                sp.wait_ge(out_ready, 4 * (NBLK - 1) + 2 * (f + 1))
                sp.dma_start(out_dram[NBLK - 1, :, f, :], x1T[:, f, :]).then_inc(out_stored, 16)
            sp.wait_ge(out_stored, 16 * (NBLK + 1))

        @block.gpsimd
        def _(pool):
            def inv_sqrt(out, arg, n, ready):
                pool.tensor_tensor(out, arg, neg_half[:, 0:n], ALU.pow).then_inc(ready, 1)

            def a_lo_part(q, k):
                pool.wait_ge(a_ready, q + 1)
                pool.wait_ge(ahi_ready, q + 1)
                pool.tensor_tensor(a_lo[:, k % NAB, :], act[:, k % NACT, :], a_hi[:, k % NAB, :].bitcast(F32),
                                   ALU.subtract).then_inc(alo_ready, 1)

            def ln1_scale(n):
                pool.wait_ge(var1_ready, n + 1)
                inv_sqrt(rstd1[:, :], var1[:, :], TILES, rstd1_ready)

            def rms_scale(n):
                pool.wait_ge(ms_ready, n + 1)
                inv_sqrt(r1[:, :], ms[:, :], TILES, r1_ready)

            def ln2_scale(i, e):
                pool.wait_ge(var2_ready, BPB * i + e + 1)
                t = slice(TPB * e, TPB * e + TPB)
                inv_sqrt(rstd2[:, t], var2[:, t], TPB, rstd2_ready)

            def qk_scale(n, e):
                pool.wait_ge(arg_ready, 2 * (BPB * n + e) + 2)
                a = qk_arg[:, :, :].rearrange("p t s -> p (t s)")
                r = rqk[:, :, :].rearrange("p t s -> p (t s)")
                w = 2 * TPB
                inv_sqrt(r[:, w * e:w * e + w], a[:, w * e:w * e + w], w, rqk_ready)

            def ww_lo_part(n, e):
                for t in range(TPB):
                    tile = TPB * e + t
                    pool.wait_ge(wv_ready, TILES * n + tile + 1)
                    pool.wait_ge(wwhi_ready, TILES * n + tile + 1)
                    pool.tensor_tensor(ww_lo[:, t, :], tok[:, tile, D:3 * D], ww_hi[:, t, :].bitcast(F32),
                                       ALU.subtract).then_inc(wwlo_ready, 1)

            def body(i, last=False):
                n = i + 1
                for j in range(HT):
                    if j < HT - 1:
                        a_lo_part(PAIRS * i + j, j)
                    if not last:
                        if j == 0:
                            ln1_scale(n)
                        if j == 3:
                            rms_scale(n)
                ln2_scale(i, 0)
                ln2_scale(i, 1)
                if not last:
                    qk_scale(n, 0)
                    ww_lo_part(n, 0)
                    qk_scale(n, 1)
                for j in range(HT, PAIRS):
                    if j == 10 and not last:
                        ww_lo_part(n, 1)
                    if j < PAIRS - 1 or not last:
                        a_lo_part(PAIRS * i + j, j)

            pool.memset(neg_half[:, :], -0.5)
            pool.memset(ident[:, :], 0.0).then_inc(cst_made, 1)
            pool.memset(hy[:, 0, 0:2 * P], 1.0).then_inc(cst_made, 1)
            pool.wait_ge(cst_made, 2)
            pool.affine_select(out=ident[:, :], in_=ident[:, :], compare_op=ALU.not_equal, fill=1.0,
                               base=0, pattern=[[-1, P]], channel_multiplier=1).then_inc(cst_made, 1)
            pool.affine_select(out=hy[:, 0, P:2 * P], in_=hy[:, 0, P:2 * P], compare_op=ALU.is_ge, fill=0.0,
                               base=0, pattern=[[1, P]], channel_multiplier=-1).then_inc(cst_made, 1)
            for c in range(NCH_QKV):
                if c == 1:
                    ln1_scale(0)
                pool.wait_ge(whi_ready, c + 1)
                pool.tensor_tensor(w_lo[:, c * CH:(c + 1) * CH], stage[:, c % NST, :],
                                   w_hi[:, c * CH:(c + 1) * CH].bitcast(F32), ALU.subtract).then_inc(qkvlo_ready, 1)
            rms_scale(0)
            qk_scale(0, 0)
            qk_scale(0, 1)
            for t in range(TPB, TILES):
                pool.wait_ge(w_ready, t + 1)
                pool.wait_ge(v_out, t + 1)
                pool.tensor_tensor(tok[:, t, 2 * D:3 * D], tok[:, t, 2 * D:3 * D], tok[:, t, D:2 * D],
                                   ALU.mult).then_inc(wv_ready, 1)
            ww_lo_part(0, 1)
            body(0)
            with pool.Fori(1, NBLK - 1) as i:
                body(i)
            body(NBLK - 1, True)

        @block.scalar
        def _(se):
            def split_hi(c):
                se.wait_ge(st_loaded[c % NST], 16 * (c // NST + 1))
                se.activation(w_hi[:, c * CH:(c + 1) * CH], stage[:, c % NST, :], ACT.Copy).then_inc(whi_ready, 1)

            def a_hi_part(q, k):
                se.wait_ge(a_ready, q + 1)
                se.activation(a_hi[:, k % NAB, :], act[:, k % NACT, :], ACT.Copy).then_inc(ahi_ready, 1)

            def tanh(q, k):
                se.wait_ge(pair_ps, q + 1)
                if not isinstance(q, int) or q > 1:
                    se.wait_ge(alo_ready, q - 1)
                se.activation(act[:, k % NACT, :], gt_ps[k % 2][:, :], ACT.Tanh,
                              scale=0.25 if k % PAIRS < HT else 0.5).then_inc(th_ready, 1)

            def h_squares(n, e):
                for t in range(TPB * e, TPB * e + TPB):
                    se.wait_ge(h_done, TILES * n + t + 1)
                    if t > 1:
                        se.wait_ge(hsq_ready, TILES * n + t - 1)
                    elif later(n):
                        se.wait_ge(sq_done, 2 * TILES * n)
                    se.activation(junk[:, t % 2, :], hy[:, t, :], ACT.Square,
                                  accum_out=hsq[:, t:t + 1]).then_inc(hsq_ready, 1)

            def hT_hi_part(n, e):
                se.wait_ge(hT_ps, BPB * n + e + 1)
                se.activation(hT_hi[:, :, cols(e)], by_feat(mps[e]), ACT.Copy).then_inc(hThi_ready, 1)

            def qk_out_part(n, t):
                se.wait_ge(qk_ps, TILES * n + t + 1)
                if t == 0:
                    if later(n):
                        se.wait_ge(y_ready, TILES * n)
                    se.wait_ge(hsq_ready, TILES * (n + 1))
                se.activation(tok[:, t, 0:2 * D], up_ps[t % 2][:, :], ACT.Copy).then_inc(qk_out, 1)

            def v_out_part(n, t):
                se.wait_ge(v_ps, TILES * n + t + 1)
                if t == 0:
                    se.wait_ge(r1_ready, n + 1)
                se.activation(tok[:, t, 2 * D:3 * D], gt_ps[t % 2][:, 0:D], ACT.Copy,
                              scale=r1[:, t:t + 1]).then_inc(v_out, 1)

            def qk_copy(n, t):
                qk_out_part(n, t)
                v_out_part(n, t)

            def qk_squares(n, t):
                se.wait_ge(qk_out, TILES * n + t + 1)
                for s in range(2):
                    if t > 0:
                        se.wait_ge(sq_done, 2 * (TILES * n + t) - 1 + s)
                    se.activation(junk[:, s, :], tok[:, t, s * D:(s + 1) * D], ACT.Square,
                                  accum_out=qk_sq[:, t, s:s + 1]).then_inc(sq_done, 1)

            def exp_part(n, t):
                se.wait_ge(rqk_ready, BPB * n + t // TPB + 1)
                se.wait_ge(sq_done, 2 * (TILES * n + t + 1))
                se.activation(tok[:, t, D:2 * D], tok[:, t, D:2 * D], ACT.Exp,
                              scale=rqk[:, t, 1:2]).then_inc(w_ready, 1)

            def tanh_q_part(n, t):
                se.activation(tok[:, t, 0:D], tok[:, t, 0:D], ACT.Tanh,
                              scale=rqk[:, t, 0:1]).then_inc(thq_ready, 1)

            def exp_tanh(n, t):
                exp_part(n, t)
                tanh_q_part(n, t)

            def ww_hi_part(n, e):
                if e:
                    se.wait_ge(cum_ps, TILES * n + TPB)
                for t in range(TPB):
                    tile = TPB * e + t
                    se.wait_ge(wv_ready, TILES * n + tile + 1)
                    se.activation(ww_hi[:, t, :], tok[:, tile, D:3 * D], ACT.Copy).then_inc(wwhi_ready, 1)

            def den_part(n, t):
                se.wait_ge(cum_ps, TILES * n + t + 1)
                if t > 1:
                    se.wait_ge(y_ready, TILES * n + t - 1)
                se.activation(den[:, t % 2, :], cum_bank(n, t)[:, 0:D], ACT.Copy,
                              bias=EPS_DEN).then_inc(den_ready, 1)

            def yT_hi_part(n, e):
                se.wait_ge(yT_ps, BPB * n + e + 1)
                se.activation(yT_hi[:, :, cols(e)], by_feat(mps[e]), ACT.Copy).then_inc(yThi_ready, 1)

            def h2T_hi_part(i, e):
                se.wait_ge(h2T_ps, BPB * i + e + 1)
                se.activation(hT_hi[:, :, cols(e)], by_feat(acc[e]), ACT.Copy).then_inc(h2Thi_ready, 1)

            def body(i, last=False):
                n = i + 1
                q = PAIRS * i
                for j in range(1, HT):
                    tanh(q + j, j)
                    if not last:
                        if j in (3, 4):
                            h_squares(n, j - 3)
                        if j in (5, 6):
                            hT_hi_part(n, j - 5)
                    a_hi_part(q + j, j)
                    if not later(i):
                        for c in SPLIT_AT.get(j, ()):
                            split_hi(c)
                if not last:
                    qk_copy(n, 0)
                    qk_squares(n, 0)
                    qk_copy(n, 1)
                h2T_hi_part(i, 0)
                if not last:
                    qk_squares(n, 1)
                    qk_copy(n, 2)
                    exp_part(n, 0)
                    exp_part(n, 1)
                    qk_copy(n, 3)
                h2T_hi_part(i, 1)
                if not last:
                    ww_hi_part(n, 0)
                    qk_squares(n, 2)
                    qk_squares(n, 3)
                for j in range(HT, PAIRS):
                    tanh(q + j, j)
                    if not last:
                        if j == 8:
                            tanh_q_part(n, 0)
                            tanh_q_part(n, 1)
                        if j == 9:
                            exp_tanh(n, 2)
                            exp_tanh(n, 3)
                        if j in (9, 12):
                            den_part(n, 2 * (j // 12))
                            den_part(n, 2 * (j // 12) + 1)
                        if j == 9:
                            ww_hi_part(n, 1)
                    a_hi_part(q + j, j)
                    if not last:
                        if j in (14, 15):
                            yT_hi_part(n, j - 14)
                    if not later(i):
                        for c in SPLIT_AT.get(j, ()):
                            split_hi(c)
                if not last:
                    tanh(q + PAIRS, PAIRS)
                    a_hi_part(q + PAIRS, PAIRS)

            se.wait_ge(c_loaded, 16)
            se.activation(c_th[:, :, :], c_sb[:, :, :], ACT.Tanh, scale=0.5).then_inc(cth_ready, 1)
            for e in range(BPB):
                for c in ([0], [1, 2])[e]:
                    split_hi(c)
                se.wait_ge(rep_ps, e + 1)
                se.activation(rows[:, e, D:2 * D], up_ps[e][:, D:2 * D], ACT.Copy, scale=0.5,
                              bias=1.0).then_inc(rep_ready, 1)
                se.activation(rows[:, e, 0:D], up_ps[e][:, 0:D], ACT.Copy, scale=0.5).then_inc(rep_ready, 1)
            hT_hi_part(0, 0)
            h_squares(0, 0)
            hT_hi_part(0, 1)
            h_squares(0, 1)
            for c in range(3, 6):
                split_hi(c)
            for t in range(3):
                qk_out_part(0, t)
                qk_squares(0, t)
            qk_out_part(0, 3)
            exp_part(0, 0)
            exp_part(0, 1)
            qk_squares(0, 3)
            ww_hi_part(0, 0)
            den_part(0, 0)
            exp_part(0, 2)
            exp_part(0, 3)
            tanh_q_part(0, 0)
            den_part(0, 1)
            tanh_q_part(0, 1)
            ww_hi_part(0, 1)
            tanh_q_part(0, 2)
            tanh_q_part(0, 3)
            den_part(0, 2)
            den_part(0, 3)
            yT_hi_part(0, 0)
            for c in range(6, 9):
                split_hi(c)
            yT_hi_part(0, 1)
            tanh(0, 0)
            a_hi_part(0, 0)
            body(0)
            with se.Fori(1, NBLK - 1) as i:
                body(i)
            body(NBLK - 1, True)

        @block.vector
        def _(ve):
            def split_lo(c):
                ve.wait_ge(whi_ready, c + 1)
                ve.tensor_tensor(w_lo[:, c * CH:(c + 1) * CH], stage[:, c % NST, :],
                                 w_hi[:, c * CH:(c + 1) * CH].bitcast(F32), ALU.subtract).then_inc(wlo_ready, 1)

            def pair(q, k):
                a = act[:, k % NACT, :]
                ve.wait_ge(th_ready, q + 1)
                ve.scalar_tensor_tensor(out=a, in0=a, scalar=1.0, in1=gt_ps[k % 2][:, :],
                                        op0=ALU.add, op1=ALU.mult).then_inc(tg_done, 1)
                ve.wait_ge(tg_done, q + 1)
                ve.tensor_tensor(a, a, up_ps[k % 2][:, :], ALU.mult).then_inc(a_ready, 1)

            def a_lo_part(q, k):
                ve.wait_ge(ahi_ready, q + 1)
                ve.wait_ge(alo_ready, q)
                ve.tensor_tensor(a_lo[:, k % NAB, :], act[:, k % NACT, :], a_hi[:, k % NAB, :].bitcast(F32),
                                 ALU.subtract).then_inc(alo_ready, 1)

            def ln1_stats(n):
                ve.wait_ge(x_loaded, 16 * (n + 1))
                for t in range(TILES):
                    ve.bn_stats(bn1[:, t, :], x_sb[:, t, :]).then_inc(bn1_done, 1)
                ve.wait_ge(bn1_done, TILES * (n + 1))
                ve.sem_inc(stats_seen, 1)
                for t in range(TILES):
                    ve.bn_aggr(mv1[:, t, :], bn1[:, t, :]).then_inc(mv1_done, 1)
                ve.wait_ge(mv1_done, TILES * n + TILES)
                ve.tensor_scalar(var1[:, :], mv1[:, :, 1], EPS_LN, None, ALU.add).then_inc(var1_ready, 1)

            def ln1_h(n, e):
                if e == 0:
                    if later(n):
                        ve.wait_ge(rows1_loaded, 16 * n)
                if not later(n):
                    ve.wait_ge(rep_ready, 2 * e + 2)
                    if later(n):
                        ve.wait_ge(yT_ps, BPB * n)
                for t in range(TPB * e, TPB * e + TPB):
                    ve.scalar_tensor_tensor(out=hy[:, t, :], in0=x_sb[:, t, :], scalar=mv1[:, t, 0:1],
                                            in1=rows[:, e, D:2 * D], op0=ALU.subtract,
                                            op1=ALU.mult).then_inc(h_part, 1)
                ve.wait_ge(rstd1_ready, n + 1)
                for t in range(TPB * e, TPB * e + TPB):
                    ve.wait_ge(h_part, TILES * n + t + 1)
                    ve.scalar_tensor_tensor(out=hy[:, t, :], in0=hy[:, t, :], scalar=rstd1[:, t:t + 1],
                                            in1=rows[:, e, 0:D], op0=ALU.mult, op1=ALU.add).then_inc(h_done, 1)

            def rms_prep(n):
                ve.wait_ge(hsq_ready, TILES * (n + 1))
                ve.tensor_scalar(ms[:, :], hsq[:, :], 1.0 / D, EPS_RMS, ALU.mult, ALU.add).then_inc(ms_ready, 1)
                ve.wait_ge(ms_ready, n + 1)
                ve.tensor_scalar(ems[:, :, 0], ms[:, :], 4 * EPS_RMS, None, ALU.mult).then_inc(ems_ready, 1)
                ve.tensor_scalar(ems[:, :, 1], ms[:, :], EPS_RMS, None, ALU.mult).then_inc(ems_ready, 1)

            def hT_lo_part(n, e):
                ve.wait_ge(hThi_ready, BPB * n + e + 1)
                ve.tensor_tensor(hT_lo[:, :, cols(e)], by_feat(mps[e]), hT_hi[:, :, cols(e)].bitcast(F32),
                                 ALU.subtract).then_inc(hTlo_ready, 1)

            def base_part(n, e):
                if e == 0:
                    ve.wait_ge(xT_loaded, 16 * (n + 1))
                for f in range(KD):
                    b = base[:, n % 2, f, cols(e)]
                    last = ve.scalar_tensor_tensor(out=b, in0=by_feat(mps[e])[:, f, :], scalar=gate_of(gates, f, n, e),
                                                   in1=b, op0=ALU.mult, op1=ALU.add)
                last.then_inc(base_done, 1)

            def gate_of(g, m, n, e):
                if isinstance(n, int):
                    return g[:, m, BPB * n + e:BPB * n + e + 1]
                return g[:, m, bass.ds(BPB * n + e, 1)]

            def qk_args(n, e):
                t = slice(TPB * e, TPB * e + TPB)
                ve.wait_ge(sq_done, 2 * (TILES * n + TPB * e + TPB))
                ve.wait_ge(ems_ready, 2 * n + 2)
                for s, f in ((0, 4.0), (1, 1.0)):
                    ve.scalar_tensor_tensor(out=qk_arg[:, t, s], in0=qk_sq[:, t, s], scalar=f / D,
                                            in1=ems[:, t, s], op0=ALU.mult, op1=ALU.add).then_inc(arg_ready, 1)

            def v_part(n, t):
                ve.wait_ge(v_ps, TILES * n + t + 1)
                if t == 0:
                    ve.wait_ge(r1_ready, n + 1)
                ve.tensor_scalar(tok[:, t, 2 * D:3 * D], gt_ps[t % 2][:, 0:D], r1[:, t:t + 1], None,
                                 ALU.mult).then_inc(v_out, 1)

            def wv_part(n, t):
                ve.wait_ge(w_ready, TILES * n + t + 1)
                ve.wait_ge(v_out, TILES * n + t + 1)
                ve.tensor_tensor(tok[:, t, 2 * D:3 * D], tok[:, t, 2 * D:3 * D], tok[:, t, D:2 * D],
                                 ALU.mult).then_inc(wv_ready, 1)

            def ww_lo_part(n, e):
                for t in range(TPB):
                    tile = TPB * e + t
                    ve.wait_ge(wwhi_ready, TILES * n + tile + 1)
                    ve.tensor_tensor(ww_lo[:, t, :], tok[:, tile, D:3 * D], ww_hi[:, t, :].bitcast(F32),
                                     ALU.subtract).then_inc(wwlo_ready, 1)

            def rec_part(n, t):
                d = den[:, t % 2, :]
                ve.wait_ge(den_ready, TILES * n + t + 1)
                ve.reciprocal(d, d).then_inc(rec_done, 1)

            def y_part(n, t, reciprocal=True):
                d = den[:, t % 2, :]
                if reciprocal:
                    rec_part(n, t)
                ve.wait_ge(rec_done, TILES * n + t + 1)
                ve.tensor_tensor(d, d, cum_bank(n, t)[:, D:2 * D], ALU.mult).then_inc(cum_used, 1)
                ve.wait_ge(cum_used, TILES * n + t + 1)
                ve.wait_ge(thq_ready, TILES * n + t + 1)
                ve.scalar_tensor_tensor(out=hy[:, t, :], in0=tok[:, t, 0:D], scalar=1.0, in1=d,
                                        op0=ALU.add, op1=ALU.mult).then_inc(y_ready, 1)

            def yT_lo_part(n, e):
                ve.wait_ge(yThi_ready, BPB * n + e + 1)
                ve.tensor_tensor(yT_lo[:, :, cols(e)], by_feat(mps[e]), yT_hi[:, :, cols(e)].bitcast(F32),
                                 ALU.subtract).then_inc(yTlo_ready, 1)

            def x1_part(i):
                if later(i):
                    ve.wait_ge(out_stored, 16 * i)
                for f in range(KD):
                    ve.wait_ge(acc_done, 2 * KD * i + f + 1)
                    for e in range(BPB):
                        ve.scalar_tensor_tensor(out=x1T[:, f, cols(e)], in0=acc[f][:, cols(e)],
                                                scalar=gate_of(gates_s, f, i, e),
                                                in1=base[:, i % 2, f, cols(e)],
                                                op0=ALU.mult, op1=ALU.add).then_inc(x1_ready, 1)

            def ln2_stats(i, e):
                ve.wait_ge(x1_ps, BPB * i + e + 1)
                ts = range(TPB * e, TPB * e + TPB)
                for t in ts:
                    ve.bn_stats(bn2[:, t, :], by_tile(mps[e])[:, t % TPB, :]).then_inc(bn2_done, 1)
                ve.wait_ge(bn2_done, TILES * i + TPB * e + TPB)
                ve.sem_inc(stats_seen, 1)
                for t in ts:
                    ve.bn_aggr(mv2[:, t, :], bn2[:, t, :]).then_inc(mv2_done, 1)
                ve.wait_ge(mv2_done, TILES * i + TPB * e + TPB)
                t = slice(TPB * e, TPB * e + TPB)
                ve.tensor_scalar(var2[:, t], mv2[:, t, 1], EPS_LN, None, ALU.add).then_inc(var2_ready, 1)

            def ln2_scaled(i, e):
                if e == 0:
                    ve.wait_ge(rows2_loaded, 16 * (i + 1))
                for t in range(TPB * e, TPB * e + TPB):
                    ve.scalar_tensor_tensor(out=hy[:, t, :], in0=by_tile(mps[e])[:, t % TPB, :],
                                            scalar=mv2[:, t, 0:1], in1=rows[:, e, D:2 * D],
                                            op0=ALU.subtract, op1=ALU.mult).then_inc(h2_part, 1)

            def ln2_h(i, e):
                ve.wait_ge(rstd2_ready, BPB * i + e + 1)
                for t in range(TPB * e, TPB * e + TPB):
                    ve.wait_ge(h2_part, TILES * i + t + 1)
                    ve.scalar_tensor_tensor(out=hy[:, t, :], in0=hy[:, t, :], scalar=rstd2[:, t:t + 1],
                                            in1=rows[:, e, 0:D], op0=ALU.mult, op1=ALU.add).then_inc(h2_done, 1)

            def h2T_lo_part(i, e):
                ve.wait_ge(h2Thi_ready, BPB * i + e + 1)
                ve.tensor_tensor(hT_lo[:, :, cols(e)], by_feat(acc[e]), hT_hi[:, :, cols(e)].bitcast(F32),
                                 ALU.subtract).then_inc(h2Tlo_ready, 1)

            def out_part(i):
                for f in range(KD):
                    ve.wait_ge(acc_done, 2 * KD * i + KD + f + 1)
                    for e in range(BPB):
                        o = x1T[:, f, cols(e)]
                        ve.scalar_tensor_tensor(out=o, in0=acc[f][:, cols(e)],
                                                scalar=gate_of(gates_s, KD + f, i, e), in1=o,
                                                op0=ALU.mult, op1=ALU.add).then_inc(out_ready, 1)

            def body(i, last=False):
                n = i + 1
                q = PAIRS * i
                for j in range(1, HT):
                    pair(q + j, j)
                    if not last:
                        if j == 1:
                            ln1_stats(n)
                        if j in (2, 3):
                            ln1_h(n, j - 2)
                        if j == 4:
                            rms_prep(n)
                        if j in (5, 6):
                            hT_lo_part(n, j - 5)
                            base_part(n, j - 5)
                    if not later(i) and j < HT - 1:
                        for c in SPLIT_AT.get(j, ()):
                            split_lo(c)
                a_lo_part(q + HT - 1, HT - 1)
                x1_part(i)
                ln2_stats(i, 0)
                ln2_scaled(i, 0)
                ln2_h(i, 0)
                ln2_stats(i, 1)
                if not last:
                    ln2_scaled(i, 1)
                    qk_args(n, 0)
                h2T_lo_part(i, 0)
                if last:
                    ln2_scaled(i, 1)
                ln2_h(i, 1)
                if not last:
                    wv_part(n, 0)
                    wv_part(n, 1)
                h2T_lo_part(i, 1)
                if not later(i):
                    for c in SPLIT_AT[HT - 1]:
                        split_lo(c)
                if not last:
                    qk_args(n, 1)
                for j in range(HT, PAIRS):
                    pair(q + j, j)
                    if not last:
                        if j == 9:
                            wv_part(n, 2)
                            wv_part(n, 3)
                        if j == 9:
                            rec_part(n, 0)
                        if j == 10:
                            y_part(n, 0, reciprocal=False)
                            y_part(n, 1)
                        if j in (12, 13):
                            y_part(n, j - 10)
                        if j in (14, 15):
                            yT_lo_part(n, j - 14)
                    if not later(i):
                        for c in SPLIT_AT.get(j, ()):
                            split_lo(c)
                if last:
                    a_lo_part(q + PAIRS - 1, PAIRS - 1)
                else:
                    pair(q + PAIRS, PAIRS)
                out_part(i)

            ve.wait_ge(cth_ready, 1)
            for k in range(KD):
                ve.scalar_tensor_tensor(
                    out=c_rep[:, k, :, :], in0=c_th[:, k, 0:BPB].unsqueeze(2).to_broadcast([P, BPB, P]),
                    scalar=1.0, in1=c_sb[:, k, 0:BPB].unsqueeze(2).to_broadcast([P, BPB, P]),
                    op0=ALU.add, op1=ALU.mult).then_inc(crep_ready, 1)
            ve.wait_ge(crep_ready, KD)
            ve.scalar_tensor_tensor(out=c_th[:, :, :], in0=c_th[:, :, :], scalar=1.0, in1=c_sb[:, :, :],
                                    op0=ALU.add, op1=ALU.mult).then_inc(silu_ready, 1)
            ve.wait_ge(cst_made, 4)
            ve.tensor_copy(ones[:, :], hy[:, 0, 0:P]).then_inc(cst_ready, 1)
            ve.tensor_copy(tri[:, :], hy[:, 0, P:2 * P]).then_inc(cst_ready, 1)
            ve.wait_ge(cst_ready, 2)
            ln1_stats(0)
            ln1_h(0, 0)
            ln1_h(0, 1)
            hT_lo_part(0, 0)
            hT_lo_part(0, 1)
            rms_prep(0)
            for c in range(3, 6):
                split_lo(c)
                if c == 4:
                    v_part(0, 0)
            ve.wait_ge(gate_ps, 1)
            ve.tensor_scalar(gate_raw[:, :, :].rearrange("p m b -> p (m b)"), acc[0][:, 0:2 * KD * NBATCH],
                             0.5, None, ALU.mult).then_inc(mod_step, 1)
            ve.wait_ge(mod_step, 1)
            ve.tensor_scalar(gate_sgn[:, :, :], gate_raw[:, :, :], 0.0, 2.0, ALU.is_ge,
                             ALU.mult).then_inc(mod_step, 1)
            ve.scalar_tensor_tensor(out=gate_abs[:, :, :], in0=gate_raw[:, :, :], scalar=-1.0,
                                    in1=gate_raw[:, :, :], op0=ALU.mult, op1=ALU.max).then_inc(mod_step, 1)
            ve.wait_ge(mod_step, 3)
            ve.tensor_scalar(gate_abs[:, :, :], gate_abs[:, :, :], 0.25, None, ALU.max).then_inc(mod_step, 1)
            ve.wait_ge(mod_step, 4)
            ve.scalar_tensor_tensor(out=gates[:, :, :], in0=gate_sgn[:, :, :], scalar=-1.0,
                                    in1=gate_abs[:, :, :], op0=ALU.add, op1=ALU.mult).then_inc(mod_step, 1)
            ve.wait_ge(mod_step, 5)
            ve.tensor_scalar(gates_s[:, 0:KD, :], gates[:, 0:KD, :], 1.0 / 8, None, ALU.mult).then_inc(gates_ready, 1)
            ve.tensor_scalar(gates_s[:, KD:, :], gates[:, KD:, :], 0.5, None, ALU.mult).then_inc(gates_ready, 1)
            ve.wait_ge(gates_ready, 2)
            v_part(0, 1)
            qk_args(0, 0)
            base_part(0, 0)
            base_part(0, 1)
            v_part(0, 2)
            v_part(0, 3)
            wv_part(0, 0)
            wv_part(0, 1)
            qk_args(0, 1)
            ww_lo_part(0, 0)
            y_part(0, 0)
            y_part(0, 1)
            y_part(0, 2)
            yT_lo_part(0, 0)
            y_part(0, 3)
            split_lo(6)
            yT_lo_part(0, 1)
            for r in range(2):
                ve.wait_ge(mod_ps, r + 1)
                a = acc[1 - r]
                ve.tensor_scalar(rows_sb[:, r, 0:D], a[0:NBATCH, 0:D], 0.5, None, ALU.mult).then_inc(mod_step, 1)
                ve.tensor_scalar(rows_sb[:, r, D:2 * D], a[0:NBATCH, D:2 * D], 0.5, 1.0,
                                 ALU.mult, ALU.add).then_inc(mod_step, 1)
                ve.wait_ge(mod_step, 5 + 2 * r + 2)
                ve.engine_nop().then_inc(rows_ready, 1)
            split_lo(7)
            pair(0, 0)
            split_lo(8)
            body(0)
            with ve.Fori(1, NBLK - 1) as i:
                body(i)
            body(NBLK - 1, True)

        @block.tensor
        def _(pe):
            def product(out, terms):
                for k, (c, hi, lo) in enumerate(terms):
                    end = k == len(terms) - 1
                    pe.matmul(out, w_hi[:, c:c + P], hi, start=k == 0, stop=False)
                    pe.matmul(out, w_hi[:, c:c + P], lo, start=False, stop=False)
                    last = pe.matmul(out, w_lo[:, c:c + P], hi, start=False, stop=end)
                return last

            def half_pair(w0, j, hi, lo, tk):
                for h, ps in ((0, up_ps[j % 2]), (1, gt_ps[j % 2])):
                    last = product(ps[:, tk], [(in_col(w0, j, h, f), hi[:, f, tk], lo[:, f, tk]) for f in range(KD)])
                return last

            def S_half(i, j, e):
                pe.wait_ge(yThi_ready, BPB * i + e + 1)
                pe.wait_ge(yTlo_ready, BPB * i + e + 1)
                last = half_pair(MIX0, j, yT_hi, yT_lo, cols(e))
                if e == BPB - 1:
                    last.then_inc(pair_ps, 1)

            def S(i, j):
                if later(i) or j > 1:
                    pe.wait_ge(a_ready, PAIRS * i + j - 1)
                if j == 0:
                    S_half(i, 0, 0)
                    S_half(i, 0, 1)
                    return
                if not later(i):
                    wait_weights(pe, in_col(MIX0, j, 1, KD - 1) + P)
                half_pair(MIX0, j, yT_hi, yT_lo, slice(0, TOK)).then_inc(pair_ps, 1)

            def G_half(i, j, e):
                pe.wait_ge(h2Thi_ready, BPB * i + e + 1)
                pe.wait_ge(h2Tlo_ready, BPB * i + e + 1)
                last = half_pair(FFN0, j, hT_hi, hT_lo, cols(e))
                if e == BPB - 1:
                    last.then_inc(pair_ps, 1)

            def G_first(i, more):
                if not later(i):
                    wait_weights(pe, in_col(FFN0, 1, 1, KD - 1) + P)
                for j in (0, 1):
                    if more:
                        pe.wait_ge(qk_out, TILES * (i + 1) + j + 3)
                        pe.wait_ge(v_out, TILES * (i + 1) + j + 3)
                    else:
                        pe.wait_ge(a_ready, PAIRS * i + HT + j - 1)
                    G_half(i, j, 0)
                    if j == 0 and not more:
                        N(i, 1)
                G_half(i, 0, 1)
                G_half(i, 1, 1)

            def G(i, j):
                if not later(i):
                    wait_weights(pe, in_col(FFN0, j, 1, KD - 1) + P)
                pe.wait_ge(a_ready, PAIRS * i + HT + j - 1)
                half_pair(FFN0, j, hT_hi, hT_lo, slice(0, TOK)).then_inc(pair_ps, 1)

            def project(i, j, ph, w0):
                q = PAIRS * i + ph * HT + j
                if not later(i):
                    wait_weights(pe, out_col(w0, j, KD - 1) + P)
                    if j == 0 and ph == 0:
                        pe.wait_ge(mod_step, 9)
                elif j == 0 and ph == 0:
                    pe.wait_ge(out_ready, 4 * i)
                pe.wait_ge(ahi_ready, q + 1)
                pe.wait_ge(alo_ready, q + 1)
                hi, lo = a_hi[:, j % NAB, :], a_lo[:, j % NAB, :]
                for f in range(KD):
                    c = out_col(w0, j, f)
                    pe.matmul(acc[f][:, :], w_hi[:, c:c + P], hi, start=j == 0, stop=False)
                    pe.matmul(acc[f][:, :], w_hi[:, c:c + P], lo, start=False, stop=False)
                    last = pe.matmul(acc[f][:, :], w_lo[:, c:c + P], hi, start=False, stop=j == HT - 1)
                    if j == HT - 1:
                        last.then_inc(acc_done, 1)

            def O(i, j):
                project(i, j, 0, MIX0)

            def Dn(i, j):
                project(i, j, 1, FFN0)

            def token_to_feature(dst, e, ready):
                for t in range(TPB):
                    for f in range(KD):
                        last = pe.transpose(by_feat(dst)[:, f, t * P:(t + 1) * P],
                                            hy[:, TPB * e + t, f * P:(f + 1) * P], ident[:, :])
                last.then_inc(ready, 1)

            def A(n, e):
                pe.wait_ge(h_done, TILES * n + TPB * (e + 1))
                token_to_feature(mps[e], e, hT_ps)

            def X(i, e):
                pe.wait_ge(x1_ready, 4 * i + 3 + e)
                for t in range(TPB):
                    for f in range(KD):
                        last = pe.transpose(by_tile(mps[e])[:, t, f * P:(f + 1) * P],
                                            x1T[:, f, (TPB * e + t) * P:(TPB * e + t + 1) * P], ident[:, :])
                last.then_inc(x1_ps, 1)

            def N(i, e):
                pe.wait_ge(h2_done, TILES * i + TPB * (e + 1))
                token_to_feature(acc[e], e, h2T_ps)

            def Q_part(t, out, c0, wd):
                for f in range(KD):
                    c = QKV0 + f * 3 * D + c0
                    hi, lo = hT_hi[:, f, t * P:(t + 1) * P], hT_lo[:, f, t * P:(t + 1) * P]
                    pe.matmul(out, hi, w_hi[:, c:c + wd], start=f == 0, stop=False)
                    pe.matmul(out, hi, w_lo[:, c:c + wd], start=False, stop=False)
                    last = pe.matmul(out, lo, w_hi[:, c:c + wd], start=False, stop=f == KD - 1)
                return last

            def wait_hT(n, t):
                pe.wait_ge(hThi_ready, BPB * n + t // TPB + 1)
                pe.wait_ge(hTlo_ready, BPB * n + t // TPB + 1)

            def Q_v(n, t):
                if t % TPB == 0:
                    wait_hT(n, t)
                Q_part(t, gt_ps[t % 2][:, 0:D], 2 * D, D).then_inc(v_ps, 1)

            def Q_qk(n, t):
                if t % TPB == 0:
                    wait_hT(n, t)
                Q_part(t, up_ps[t % 2][:, :], 0, 2 * D).then_inc(qk_ps, 1)

            def T(n, e):
                pe.wait_ge(wwhi_ready, TILES * n + TPB * e + 1)
                pe.wait_ge(wwlo_ready, TILES * n + TPB * e + 1)
                if e and later(n):
                    pe.wait_ge(cum_used, TILES * n + 1)
                ps = cum_bank(n, TPB * e)
                pe.matmul(ps[:, :], tri[:, :], ww_hi[:, 0, :], start=True, stop=False)
                pe.matmul(ps[:, :], tri[:, :], ww_lo[:, 0, :], start=False, stop=True).then_inc(cum_ps, 1)
                if e and later(n):
                    pe.wait_ge(cum_used, TILES * n + 2)
                ps = cum_bank(n, TPB * e + 1)
                pe.matmul(ps[:, :], ones[:, :], ww_hi[:, 0, :], start=True, stop=False)
                pe.matmul(ps[:, :], ones[:, :], ww_lo[:, 0, :], start=False, stop=False)
                pe.wait_ge(wwhi_ready, TILES * n + TPB * e + 2)
                pe.matmul(ps[:, :], tri[:, :], ww_hi[:, 1, :], start=False, stop=False)
                pe.wait_ge(wwlo_ready, TILES * n + TPB * e + 2)
                pe.matmul(ps[:, :], tri[:, :], ww_lo[:, 1, :], start=False, stop=True).then_inc(cum_ps, 1)

            def Y(n, e):
                pe.wait_ge(cum_used, TILES * n + e + (3 if later(n) else 1))
                pe.wait_ge(y_ready, TILES * n + TPB * (e + 1))
                token_to_feature(mps[e], e, yT_ps)

            def keep_clock(ps, count):
                for _ in range(count):
                    pe.matmul(ps[:, :], ones[:, :], w_hi[:, 0:CH], start=True, stop=True)

            def body(i, last=False):
                n = i + 1
                if later(i):
                    S(i, 1)
                for j in range(2, HT):
                    S(i, j)
                    if not last and j in (4, 5):
                        A(n, j - 4)
                    if j >= LAG:
                        O(i, j - LAG)
                for j in range(HT - LAG, HT):
                    O(i, j)
                if not last:
                    pe.wait_ge(a_ready, PAIRS * i + HT - 1)
                    Q_qk(n, 0)
                    pe.wait_ge(base_done, BPB * (n + 1))
                X(i, 0)
                X(i, 1)
                if not last:
                    Q_v(n, 0)
                    pe.wait_ge(a_ready, PAIRS * i + HT)
                    Q_v(n, 1)
                    Q_qk(n, 1)
                    pe.wait_ge(v_out, TILES * n + 1)
                    Q_v(n, 2)
                else:
                    pe.wait_ge(a_ready, PAIRS * i + HT - 1)
                    keep_clock(up_ps[0], 11)
                N(i, 0)
                if last:
                    keep_clock(up_ps[0], 7)
                else:
                    pe.wait_ge(qk_out, TILES * n + 1)
                    Q_qk(n, 2)
                    pe.wait_ge(qk_out, TILES * n + 2)
                    pe.wait_ge(v_out, TILES * n + 2)
                    Q_qk(n, 3)
                    Q_v(n, 3)
                    N(i, 1)
                G_first(i, not last)
                for j in range(1, HT):
                    if j > 1:
                        G(i, j)
                    if not last:
                        if j in (1, 4):
                            T(n, j // 4)
                        if j in (6, 7):
                            Y(n, j - 6)
                    if j >= LAG:
                        Dn(i, j - LAG)
                for j in range(HT - LAG, HT - 1):
                    Dn(i, j)
                if not last:
                    S(n, 0)
                Dn(i, HT - 1)

            def gates():
                pe.wait_ge(silu_ready, 1)
                pe.wait_ge(wgate_loaded, 16)
                for g in range(2 * KD):
                    for k in range(KD):
                        m = pe.matmul(acc[0][:, g * NBATCH:(g + 1) * NBATCH], wgate[:, k, g * P:(g + 1) * P],
                                      c_th[:, k, :], start=k == 0, stop=k == KD - 1)
                m.then_inc(gate_ps, 1)

            def all_rows(r):
                pe.wait_ge(wrow_loaded[r], 16)
                for k in range(KD):
                    m = pe.matmul(acc[1 - r][0:NBATCH, :], c_th[:, k, :], wrow[r][:, k, :],
                                  start=k == 0, stop=k == KD - 1)
                m.then_inc(mod_ps, 1)

            pe.wait_ge(cst_made, 2)
            for _ in range(WARMUP):
                pe.matmul(acc[1][:, 0:P], hy[:, 0, 0:P], hy[:, 0, 0:P], start=True, stop=True)
            pe.wait_ge(crep_ready, KD)
            pe.wait_ge(wrow_loaded[0], 16)
            for e in range(BPB):
                for k in range(KD):
                    m = pe.matmul(up_ps[e][:, :], c_rep[:, k, e, :], wrow[0][:, k, :], start=k == 0, stop=k == KD - 1)
                m.then_inc(rep_ps, 1)
            A(0, 0)
            gates()
            A(0, 1)
            wait_weights(pe, MIX0)
            pe.wait_ge(rep_ready, 2 * BPB)
            for t in range(TILES):
                if t > 1:
                    pe.wait_ge(qk_out, t - 1)
                Q_qk(0, t)
                if t > 1:
                    pe.wait_ge(v_out, t - 1)
                Q_v(0, t)
            all_rows(0)
            pe.wait_ge(base_done, BPB)
            T(0, 0)
            pe.wait_ge(mod_step, 1)
            all_rows(1)
            T(0, 1)
            Y(0, 0)
            pe.wait_ge(qk_out, TILES - 1)
            keep_clock(up_ps[0], 10)
            pe.wait_ge(qk_out, TILES)
            pe.wait_ge(v_out, TILES)
            wait_weights(pe, in_col(MIX0, 1, 1, KD - 1) + P)
            S_half(0, 0, 0)
            Y(0, 1)
            pe.wait_ge(cum_used, TILES)
            S_half(0, 1, 0)
            S_half(0, 0, 1)
            S_half(0, 1, 1)
            body(0)
            with pe.Fori(1, NBLK - 1) as i:
                body(i)
            body(NBLK - 1, True)


def kernel(L0_attn_x, L0_attn_w_qkv, L0_attn_w_swiglu, L0_attn_w_out, L0_ffn_w_gate, L0_ffn_w_up,
           L0_ffn_w_down, L0_c, L0_wmod):
    import numpy as np
    import concourse.bacc as bacc
    from concourse.bass_utils import run_bass_kernel_spmd

    def rows_by_partition(w):
        k, m = w.shape
        return w.reshape(k // P, P, m).transpose(1, 0, 2).reshape(P, -1)

    wmod = rows_by_partition(np.asarray(L0_wmod)).reshape(P, KD, 6, D)
    wmod = np.stack([wmod[:, :, part].reshape(P, KD, 2 * D) for part in ([0, 1], [3, 4], [2, 5])])
    x = np.ascontiguousarray(L0_attn_x)
    xT = x.reshape(NBLK, BPB, SEQ, KD, P).transpose(0, 4, 3, 1, 2).reshape(NBLK, P, KD, TOK)

    def hidden_groups(w_in, w_out):
        w_in = rows_by_partition(w_in.T).reshape(P, KD, 2, HT // 2, 2, P).transpose(0, 3, 4, 2, 1, 5)
        w_out = rows_by_partition(w_out.T).reshape(P, HT // 2, CH)
        return np.concatenate([w_in.reshape(P, HT // 2, 2 * CH), w_out], axis=2).reshape(P, -1)

    up_gate = np.concatenate([np.asarray(L0_ffn_w_up), np.asarray(L0_ffn_w_gate)], axis=0)
    weights = np.concatenate([
        rows_by_partition(np.asarray(L0_attn_w_qkv).T),
        hidden_groups(np.asarray(L0_attn_w_swiglu), np.asarray(L0_attn_w_out)),
        hidden_groups(up_gate, np.asarray(L0_ffn_w_down)),
    ], axis=1)
    arrays = {
        "x": x,
        "xT": np.ascontiguousarray(xT),
        "weights": np.ascontiguousarray(weights),
        "cT": np.ascontiguousarray(rows_by_partition(np.asarray(L0_c).T).reshape(P, KD, NBATCH)),
        "wmod": np.ascontiguousarray(wmod),
    }
    nc = bacc.Bacc("TRN2", target_bir_lowering=False, num_devices=1)
    args = [nc.dram_tensor(k, a.shape, mybir.dt.from_np(a.dtype), kind="ExternalInput").ap()
            for k, a in arrays.items()]
    out = nc.dram_tensor("outT", (NBLK, P, KD, TOK), F32, kind="ExternalOutput").ap()
    adaln_kernel(nc, *args, out)
    r = run_bass_kernel_spmd(nc, [arrays], core_ids=[0])
    outT = r.results[0]["outT"].reshape(NBLK, P, KD, BPB, SEQ)
    return np.ascontiguousarray(outT.transpose(0, 3, 4, 2, 1).reshape(NBATCH, SEQ, D))
```
